# Optimizing a Trainium2 kernel written in Bass

```python
import numpy as np
import jax
import jax.numpy as jnp

def _softmax(x, axis=-1):
    return jax.nn.softmax(x, axis=axis)

def _gelu(x):
    return jax.nn.gelu(x, approximate=True)

def _silu(x):
    return jax.nn.silu(x)

def _sigmoid(x):
    return jax.nn.sigmoid(x)

def _layernorm(x, axis=-1, eps=1e-05):
    m = jnp.mean(x, axis=axis, keepdims=True)
    v = jnp.var(x, axis=axis, keepdims=True)
    return (x - m) / jnp.sqrt(v + eps)

def _scatter_add(tgt, idx, src, axis=0):
    return tgt.at[idx].add(src)

def _segment_sum(src, seg, n):
    return jax.ops.segment_sum(src, seg, n)
kernel_name = 'mk_prb_d1_jaxref_r4_c28868'

def setup_inputs(seed: int=0):
    np.random.seed(seed)
    _w = jnp.asarray

    def _L0_attn_setup():
        import jax, jax.numpy as jnp
        import numpy as np
        B, S, D, H = (2, 512, 512, 16)
        HD = D // H

        def _alibi_slopes(num_heads):
            ratio = 2.0 ** (-8.0 / num_heads)
            return ratio ** jnp.arange(1, num_heads + 1, dtype=jnp.float32)
        key = jax.random.key(seed)
        ks = jax.random.split(key, 9)
        sd = 1.0 / np.sqrt(D)
        inp = {'x': jax.random.normal(ks[0], (B, S, D), dtype=jnp.float32)}
        for i, name in enumerate(['Wq', 'Wk', 'Wv', 'Wo']):
            inp[name] = jax.random.normal(ks[1 + i], (D, D), dtype=jnp.float32) * sd
        for i, name in enumerate(['bq', 'bk', 'bv', 'bo']):
            inp[name] = jax.random.normal(ks[5 + i], (D,), dtype=jnp.float32) * 0.02
        return inp
    _L0_attn_in = _L0_attn_setup()

    def _L0_ffn_setup():
        import jax, jax.numpy as jnp
        import numpy as np
        HIDDEN = 512
        INTER = 2048
        COMPRESSION = 128.9

        def _n_ctrl(out_size, in_size):
            return max(16, int(out_size * in_size / COMPRESSION))

        def _catmull_rom_grid(n_ctrl, n_samples):
            t = np.linspace(0.0, n_ctrl - 1.0, n_samples, dtype=np.float64)
            i = np.clip(np.floor(t).astype(np.int64), 0, n_ctrl - 2)
            f = (t - i).astype(np.float32)
            idx = np.stack([np.clip(i + k, 0, n_ctrl - 1) for k in (-1, 0, 1, 2)], axis=0)
            return (jnp.asarray(idx.astype(np.int32)), jnp.asarray(f))

        def spline_reconstruct(control_points, out_size, in_size):
            n = out_size * in_size
            idx, f = _catmull_rom_grid(control_points.shape[0], n)
            p0, p1, p2, p3 = (control_points[idx[0]], control_points[idx[1]], control_points[idx[2]], control_points[idx[3]])
            f2 = f * f
            f3 = f2 * f
            w = 0.5 * (2.0 * p1 + (p2 - p0) * f + (2.0 * p0 - 5.0 * p1 + 4.0 * p2 - p3) * f2 + (3.0 * p1 - p0 - 3.0 * p2 + p3) * f3)
            return w.reshape(out_size, in_size)
        key = jax.random.key(seed)
        k0, k1, k2, k3 = jax.random.split(key, 4)
        hidden_states = jax.random.normal(k0, (4, 512, HIDDEN), dtype=jnp.float32)
        gate_cp = jax.random.normal(k1, (_n_ctrl(INTER, HIDDEN),), dtype=jnp.float32) * 0.02
        up_cp = jax.random.normal(k2, (_n_ctrl(INTER, HIDDEN),), dtype=jnp.float32) * 0.02
        down_cp = jax.random.normal(k3, (_n_ctrl(HIDDEN, INTER),), dtype=jnp.float32) * 0.02
        return {'hidden_states': hidden_states, 'gate_cp': gate_cp, 'up_cp': up_cp, 'down_cp': down_cp}
    _L0_ffn_in = _L0_ffn_setup()
    _d = {'L0_attn_x': _L0_attn_in['x'], 'L0_attn_Wq': _L0_attn_in['Wq'], 'L0_attn_bq': _L0_attn_in['bq'], 'L0_attn_Wk': _L0_attn_in['Wk'], 'L0_attn_bk': _L0_attn_in['bk'], 'L0_attn_Wv': _L0_attn_in['Wv'], 'L0_attn_bv': _L0_attn_in['bv'], 'L0_attn_Wo': _L0_attn_in['Wo'], 'L0_attn_bo': _L0_attn_in['bo'], 'L0_ffn_gate_cp': _L0_ffn_in['gate_cp'], 'L0_ffn_up_cp': _L0_ffn_in['up_cp'], 'L0_ffn_down_cp': _L0_ffn_in['down_cp']}
    _x0 = _d['L0_attn_x']
    _d['L0_attn_x'] = jax.random.normal(jax.random.fold_in(jax.random.key(seed), 1), (4, 512, 512), dtype=_x0.dtype)
    del _x0
    return _d

def reference(L0_attn_x, L0_attn_Wq, L0_attn_bq, L0_attn_Wk, L0_attn_bk, L0_attn_Wv, L0_attn_bv, L0_attn_Wo, L0_attn_bo, L0_ffn_gate_cp, L0_ffn_up_cp, L0_ffn_down_cp):

    def _L0_attn_ref(x, Wq, bq, Wk, bk, Wv, bv, Wo, bo):
        import jax, jax.numpy as jnp
        import numpy as np
        B, S, D, H = (2, 512, 512, 16)
        HD = D // H

        def _alibi_slopes(num_heads):
            ratio = 2.0 ** (-8.0 / num_heads)
            return ratio ** jnp.arange(1, num_heads + 1, dtype=jnp.float32)
        b, s, d = x.shape

        def proj(W, bias):
            return (x @ W + bias).reshape(b, s, H, HD).transpose(0, 2, 1, 3)
        q, k, v = (proj(Wq, bq), proj(Wk, bk), proj(Wv, bv))
        scores = jnp.einsum('bhqd,bhkd->bhqk', q, k) / jnp.sqrt(jnp.float32(HD))
        distances = jnp.arange(1 - s, 1, dtype=jnp.float32)
        bias = _alibi_slopes(H)[None, :, None, None] * distances[None, None, None, :]
        scores = scores + bias
        causal = jnp.tril(jnp.ones((s, s), dtype=bool))[None, None]
        scores = jnp.where(causal, scores, jnp.finfo(scores.dtype).min)
        attn = jax.nn.softmax(scores, axis=-1)
        ctx = jnp.einsum('bhqk,bhkd->bhqd', attn, v)
        ctx = ctx.transpose(0, 2, 1, 3).reshape(b, s, d)
        return ctx @ Wo + bo

    def _L0_ffn_ref(hidden_states, gate_cp, up_cp, down_cp):
        import jax, jax.numpy as jnp
        import numpy as np
        HIDDEN = 512
        INTER = 2048
        COMPRESSION = 128.9

        def _n_ctrl(out_size, in_size):
            return max(16, int(out_size * in_size / COMPRESSION))

        def _catmull_rom_grid(n_ctrl, n_samples):
            t = np.linspace(0.0, n_ctrl - 1.0, n_samples, dtype=np.float64)
            i = np.clip(np.floor(t).astype(np.int64), 0, n_ctrl - 2)
            f = (t - i).astype(np.float32)
            idx = np.stack([np.clip(i + k, 0, n_ctrl - 1) for k in (-1, 0, 1, 2)], axis=0)
            return (jnp.asarray(idx.astype(np.int32)), jnp.asarray(f))

        def spline_reconstruct(control_points, out_size, in_size):
            n = out_size * in_size
            idx, f = _catmull_rom_grid(control_points.shape[0], n)
            p0, p1, p2, p3 = (control_points[idx[0]], control_points[idx[1]], control_points[idx[2]], control_points[idx[3]])
            f2 = f * f
            f3 = f2 * f
            w = 0.5 * (2.0 * p1 + (p2 - p0) * f + (2.0 * p0 - 5.0 * p1 + 4.0 * p2 - p3) * f2 + (3.0 * p1 - p0 - 3.0 * p2 + p3) * f3)
            return w.reshape(out_size, in_size)
        gate_w = spline_reconstruct(gate_cp, INTER, HIDDEN)
        up_w = spline_reconstruct(up_cp, INTER, HIDDEN)
        down_w = spline_reconstruct(down_cp, HIDDEN, INTER)
        gate = jnp.einsum('bsh,ih->bsi', hidden_states, gate_w)
        up = jnp.einsum('bsh,ih->bsi', hidden_states, up_w)
        inter = jax.nn.silu(gate) * up
        return jnp.einsum('bsi,hi->bsh', inter, down_w)
    x = L0_attn_x
    xn = _layernorm(x, axis=-1)
    x = x + _L0_attn_ref(xn, L0_attn_Wq, L0_attn_bq, L0_attn_Wk, L0_attn_bk, L0_attn_Wv, L0_attn_bv, L0_attn_Wo, L0_attn_bo) + _L0_ffn_ref(xn, L0_ffn_gate_cp, L0_ffn_up_cp, L0_ffn_down_cp)
    return x

_drawn_inputs = setup_inputs


def setup_inputs(seed=0):
    import zlib

    import numpy as np

    out = dict(_drawn_inputs(seed))
    spreads = {}
    factors = {'L0_attn_bq': 8.0, 'L0_attn_bk': 8.0, 'L0_attn_bv': 3.218, 'L0_attn_bo': 3.15}
    for name, (base, spread) in spreads.items():
        noise = np.random.default_rng([zlib.crc32(name.encode()), seed]).standard_normal(out[name].shape)
        drawn = base * np.exp(spread * noise) if base else spread * noise
        out[name] = jnp.asarray(drawn.astype(out[name].dtype))
    for name, factor in factors.items():
        out[name] = (out[name] * factor).astype(out[name].dtype)
    return out
```

```python
from contextlib import ExitStack

import numpy as np

import concourse.bass as bass
from concourse import mybir

F32 = mybir.dt.float32
F32R = mybir.dt.float32r
F16 = mybir.dt.float16
BF16 = mybir.dt.bfloat16
U8 = mybir.dt.uint8
U32 = mybir.dt.uint32
ALU = mybir.AluOpType
ACT = mybir.ActivationFunctionType
AX_X = mybir.AxisListType.X

P = 128
B, S, D = 4, 512, 512
H, HD = 16, 32
INTER = 2048
KC = D // P
HPC = P // HD
QT = S // P
EPS = 1e-5
MASKED = -3.0e38
COMPRESSION = 128.9
N_CTRL = max(16, int(INTER * D / COMPRESSION))
MATS = 3
BLOCKS = INTER * D // P
PAIRS = INTER // (2 * P)
PW = BLOCKS // PAIRS
ROLES = 3
KPOLY = 4 * ROLES
END_ROW = 32

OFF = [0, 128, 384, 768]
PROBS = 1280


def grid():
    t = np.linspace(0.0, N_CTRL - 1.0, INTER * D, dtype=np.float64)
    seg = np.clip(np.floor(t).astype(np.int64), 0, N_CTRL - 2)
    return t, seg


def block_order():
    gate = [KC * (pr * 2 * P + i) + q for pr in range(PAIRS) for q in range(KC) for i in range(2 * P)]
    down = [(INTER // P) * o + 2 * pr + j for pr in range(PAIRS) for j in range(2) for o in range(D)]
    return np.array(gate), np.array(down)


def rounded(x):
    u = np.asarray(x, np.float32).view(np.uint32)
    return ((u + 0x7FF + ((u >> 12) & 1)) & np.uint32(0xFFFFF000)).view(np.float32)


def shape_constants():
    t, seg = grid()
    delta = (N_CTRL - 1.0) / (INTER * D - 1)
    basis = np.zeros((END_ROW + KPOLY, P), np.float32)
    for row, tau in ((0, np.arange(P) * delta), (END_ROW, (np.arange(P) - (P - 1)) * delta)):
        for d in range(4):
            hi = rounded(tau**d)
            lo = rounded(tau**d - hi)
            for role, part in enumerate((hi, lo, hi)):
                basis[row + 4 * role + d] = 0.5 * part
    phase = np.zeros((P, 2, MATS, BLOCKS // P), np.float32)
    mask = np.zeros((PAIRS, P, 2, PW), np.uint8)
    for kind, order in enumerate(block_order()):
        start, end = order * P, order * P + P - 1
        at = [t[start] - seg[start], t[end] - (seg[start] + 1)]
        for m in ((0, 1), (2,))[kind]:
            for e in range(2):
                phase[:, e, m, :] = at[e].reshape(P, -1)
        behind = seg.reshape(-1, P)[order] != seg[start][:, None]
        mask[:, :, kind, :] = behind.reshape(PAIRS, PW, P).transpose(0, 2, 1)
    key = np.arange(S)
    dist = np.broadcast_to((key - (S - 1)).astype(np.float32), (P, S)).copy()
    dist[(key[None, :] - (S - P)) > np.arange(P)[:, None]] = MASKED
    return {"c_basis": basis, "c_phase": phase, "c_mask": mask.view(np.uint32), "c_dist": dist,
            "c_ident": np.eye(P, dtype=np.float32)}


def control_windows(points):
    _, seg = grid()
    out = []
    for order in block_order():
        first = seg[order * P]
        index = np.clip(first[None, :] + np.arange(-1, 4)[:, None], 0, N_CTRL - 1)
        out.append(index)
    rows = [points[m][out[0 if m < 2 else 1]] for m in range(MATS)]
    return np.ascontiguousarray(np.stack(rows).reshape(MATS, 5, P, -1).transpose(2, 1, 0, 3))


def later(b):
    return not isinstance(b, int) or b > 0


def rows_of(ap, index):
    if isinstance(index, int):
        return ap[index]
    return ap[bass.ds(index, 1)].rearrange("a p n -> (a p) n")


def build_kernel(nc, x, wq, wk, wv, wo, bq, bk, bv, bo, win, c_basis, c_phase, c_mask, c_dist, c_ident, out):
    coef_d = nc.dram_tensor("coef_scratch", (2, KPOLY, MATS, BLOCKS), F32, kind="Internal").ap()
    xt_d = nc.dram_tensor("xt_scratch", (B * 2, P, KC * S), F32, kind="Internal").ap()
    mid_d = nc.dram_tensor("mid_scratch", (B * QT, P, D), F32, kind="Internal").ap()
    x_t = x.rearrange("b (t p) d -> (b t) p d", p=P)
    out_t = out.rearrange("b (t p) d -> (b t) p d", p=P)

    with ExitStack() as outer:
        def sems(ctx, *names):
            return [ctx.enter_context(nc.semaphore(n)) for n in names]

        psum = [outer.enter_context(nc.psum_tensor(f"bank{i}", [P, 512], F32)) for i in range(8)]
        basis = outer.enter_context(nc.sbuf_tensor("basis", [END_ROW + KPOLY, P], F32R))
        attention(nc, sems, psum, basis, (wq, wk, wv, wo), bq, bk, bv, win, c_basis, c_phase, c_dist, c_ident,
                  coef_d, x_t, xt_d, mid_d)
        ffn(nc, sems, psum, basis, c_mask, coef_d, xt_d, mid_d, bo, out_t)


FRONT = [("x", t) for t in range(QT)] + [("q", 0), ("k", 0)] + [("v", t) for t in range(QT)]
BACK = [("c", 0), ("c", 1), ("o", 0), ("c", 2), ("o", 1), ("c", 3), ("o", 2), ("o", 3)]
PJ_FIRST = FRONT + [("q", 1), ("k", 1), ("q", 2), ("k", 2)]
PJ_BODY = [("q", 3), ("k", 3)] + FRONT + [("q", 1), ("k", 1)] + BACK + [("q", 2), ("k", 2)]
PJ_LAST = [("q", 3), ("k", 3)] + BACK
HALF = H // 2
W_PIECES = 8
STACK = 16 * 2 * ROLES


def pj_use(key, b):
    if not later(b) and key in PJ_FIRST:
        n = PJ_FIRST.index(key)
        return n % 2, n // 2
    n = PJ_BODY.index(key)
    own = key in FRONT or key in PJ_BODY[12:14] or key in PJ_BODY[22:]
    if not own and isinstance(b, int) and b == B - 1:
        n = PJ_LAST.index(key)
    start = len(PJ_BODY) // 2 * (b if own else b + 1) - 5
    return n % 2, start + n // 2


def pj_total(key, b):
    if not later(b) and key in PJ_FIRST:
        return PJ_FIRST.index(key) + 1
    n = PJ_BODY.index(key)
    own = key in FRONT or key in PJ_BODY[12:14] or key in PJ_BODY[22:]
    if not own and isinstance(b, int) and b == B - 1:
        n = PJ_LAST.index(key)
    return len(PJ_BODY) * (b if own else b + 1) - 10 + n + 1


def back(b, s, n):
    if s - n >= H:
        return None
    if s - n >= 0:
        return b, s - n
    return (b - 1, s - n + H) if later(b) else None


def attention(nc, sems, psum, basis, weights, bq, bk, bv, win, c_basis, c_phase, c_dist, c_ident,
              coef_d, x_t, xt_d, mid_d):
    NB = BLOCKS // P
    with ExitStack() as ctx:
        sb = lambda n, s, dt: ctx.enter_context(nc.sbuf_tensor(n, s, dt))
        w_hi = sb("w_hi", [P, 4, KC, D], F32R)
        w_lo = sb("w_lo", [P, 4, KC, D], F32R)
        dist4 = sb("dist4", [P, HPC, S], F32)
        ident = sb("ident", [P, P], F32)
        ident16 = sb("ident16", [P, P], F16)
        bv_all = sb("bv_all", [P, D], F32)
        b_qk = sb("b_qk", [P, 2, KC], F32)
        b_scaled = sb("b_scaled", [P, KC], F32)
        x_in = sb("x_in", [P, 2, D], F32)
        xn = sb("xn", [P, 2, D], F32)
        xt_hi = sb("xt_hi", [P, KC, S], F32R)
        xt_lo = sb("xt_lo", [P, KC, S], F32R)
        qk_full = sb("qk_full", [P, 2, S], F32)
        parts = sb("parts", [P, 4, S], F32R)
        q_stack = sb("q_stack", [3 * HD, 2, HPC, S], F32R)
        k_stack = sb("k_stack", [3 * HD, 2, HPC, S], F32R)
        v_full = sb("v_full", [P, QT, D], F32)
        v_parts = sb("v_parts", [P, QT, H, 3, HD], BF16)
        ctx_tmp = sb("ctx_tmp", [P, 2, QT, HD], F32)
        stats = sb("stats", [P, QT, 6], F32)
        meanvar = sb("meanvar", [P, QT, 2], F32)
        varp = sb("varp", [P, QT], F32)
        rstd = sb("rstd", [P, QT], F32)
        minus_half = sb("minus_half", [P, QT], F32)
        row_max = sb("row_max", [P, 2, QT], F32)
        neg_max = sb("neg_max", [P, 2, QT], F32)
        row_sum = sb("row_sum", [P, 4, QT], F32)
        inv_sum = sb("inv_sum", [P, 2, QT], F32)
        work = sb("work", [P, 3 * 2 * PROBS], F32)
        probs = work[:, 0:2 * PROBS].rearrange("p (s n) -> p s n", s=2)
        probs16 = work[:, 2 * PROBS:4 * PROBS].bitcast(F16).rearrange("p (s e n) -> p s e n", s=2, e=2)
        probs_t = work[:, 4 * PROBS:6 * PROBS].bitcast(F16).rearrange("p (s n) -> p s n", s=2)
        at = 3 * 2 * D
        w_raw = work[:, 0:at].rearrange("p (s c n) -> p s c n", s=3, c=2)
        points = work[:, at:at + 5 * MATS * NB].rearrange("p (k n) -> p k n", k=5)
        at += 5 * MATS * NB
        phase = work[:, at:at + 2 * MATS * NB].rearrange("p (e n) -> p e n", e=2)
        at += 2 * MATS * NB
        tmp = work[:, at:at + 8 * MATS * NB].rearrange("p (k e n) -> p k e n", k=4, e=2)
        at += 8 * MATS * NB
        poly = work[:, at:at + 8 * MATS * NB].rearrange("p (d e n) -> p d e n", d=4, e=2)
        basis_raw = ctx_tmp[0:END_ROW + KPOLY].rearrange("p a q d -> p (a q d)")[:, 0:P]
        late = sb("late", [P, 6 * D], F32)
        ctx_sb = late[:, 0:4 * D].rearrange("p (q n) -> p q n", q=QT)
        resid = late[:, 4 * D:6 * D].rearrange("p (q n) -> p q n", q=2)
        poly_hi, poly_lo = [late[:, e * 3 * D:(e + 1) * 3 * D].bitcast(F32R)
                            .rearrange("p (d e m n) -> p d e m n", d=4, e=2, m=MATS) for e in range(2)]

        pj_bank, score_bank, av_bank = psum[0:2], psum[2:4], psum[6:8]
        pt_bank = [p[:, :].bitcast(F16) for p in psum[4:6]]

        x_ld = sems(ctx, "x_ld0", "x_ld1")
        w_ld = sems(ctx, "w_ld0", "w_ld1", "w_ld2")
        pj_free = sems(ctx, "pj_free0", "pj_free1")
        pt_free = sems(ctx, "pt_free0", "pt_free1")
        stacked = sems(ctx, "stacked0", "stacked1")
        res_ld = sems(ctx, "res_ld0", "res_ld1")
        res_st = sems(ctx, "res_st0", "res_st1")
        (const_ld, points_ld, wh_ready, wl_ready, wl_pool, small_set, poly_step, ph_ready, pl_ready, coef_st,
         pj_full, ln_stats, ln_mv, ln_var, rstd_ready, xn_ready, xh_ready, xt_st,
         full_ready, ql_ready, v_rest, v_mid, vh_ready, v_done, s_full, t_done, nm_ready, p_ready, hi_ready,
         lo_ready, pt_full, av_full, av_read, ctx_ready, ch_ready) = sems(
            ctx, "const_ld", "points_ld", "wh_ready", "wl_ready", "wl_pool", "small_set", "poly_step",
            "ph_ready", "pl_ready", "coef_st", "pj_full", "ln_stats", "ln_mv",
            "ln_var", "rstd_ready", "xn_ready", "xh_ready", "xt_st", "full_ready", "ql_ready", "v_rest", "v_mid",
            "vh_ready", "v_done", "s_full", "t_done", "nm_ready", "p_ready", "p_hi_ready", "p_lo_ready",
            "pt_full", "av_full", "av_read", "ctx_ready", "ch_ready")

        block = ctx.enter_context(nc.Block())

        def w_piece(w, n):
            m, half = divmod(n, 2)
            return w[:, m, 2 * half:2 * half + 2, :]

        @block.tensor
        def _(pe):
            def turn_x(b, t):
                bank, used = pj_use(("x", t), b)
                if later(b) or used:
                    pe.wait_ge(pj_free[bank], used)
                pe.wait_ge(xn_ready, QT * b + t + 1)
                if not later(b) and t == 0:
                    pe.wait_ge(const_ld, 16 * 6)
                for c in range(KC):
                    mm = pe.transpose(pj_bank[bank][:, c * P:(c + 1) * P], xn[:, t % 2, c * P:(c + 1) * P],
                                      ident[:])
                mm.then_inc(pj_full, 1)

            def product(bank, pairs, some):
                n = len(pairs)
                mm = None
                for k in some:
                    l_hi, l_lo, r_hi, r_lo = pairs[k]
                    pe.matmul(bank[:, :], l_hi, r_hi, start=(k == 0), stop=False)
                    pe.matmul(bank[:, :], l_hi, r_lo, start=False, stop=False)
                    mm = pe.matmul(bank[:, :], l_lo, r_hi, start=False, stop=(k == n - 1))
                if some[-1] == n - 1:
                    mm.then_inc(pj_full, 1)

            def project_qk(b, name, c, some=(0, 1, 2, 3)):
                bank, used = pj_use((name, c), b)
                m = "qk".index(name)
                if some[0] == 0:
                    pe.wait_ge(pj_free[bank], used)
                    if c == 0:
                        x_bank, x_used = pj_use(("x", QT - 1 - m), b)
                        pe.wait_ge(pj_free[x_bank], x_used + 1)
                if not later(b) and c == 0:
                    pe.wait_ge(wl_ready, 2 * m + 2)
                cols = slice(c * P, (c + 1) * P)
                product(pj_bank[bank], [(w_hi[:, m, k, cols], w_lo[:, m, k, cols], xt_hi[:, k, :],
                                         xt_lo[:, k, :]) for k in range(KC)], some)

            def project_v(b, t):
                bank, used = pj_use(("v", t), b)
                pe.wait_ge(pj_free[bank], used)
                if not later(b) and t == 0:
                    pe.wait_ge(wl_pool, 2)
                rows = slice(t * P, (t + 1) * P)
                product(pj_bank[bank], [(xt_hi[:, k, rows], xt_lo[:, k, rows], w_hi[:, 2, k, :],
                                         w_lo[:, 2, k, :]) for k in range(KC)], (0, 1, 2, 3))

            def scores(b, s, i):
                c, h = divmod(s, HPC)
                if h == 0 and i == 0:
                    pe.wait_ge(stacked[c % 2], 2 * STACK * b + STACK * (c // 2 + 1))
                if later(b) or 4 * s + i >= 2:
                    pe.wait_ge(t_done, 64 * b + 4 * s + i - 1)
                n = max(2, i + 1) * P
                pe.matmul(score_bank[i % 2][:, 0:n], q_stack[:, c % 2, h, i * P:(i + 1) * P],
                          k_stack[:, c % 2, h, 0:n], start=True, stop=True).then_inc(s_full, 1)

            def turn_probs(b, s, i):
                if i == 0:
                    if not later(b) and s == 0:
                        pe.wait_ge(small_set, 2)
                    pe.wait_ge(hi_ready, H * b + s + 1)
                    pe.wait_ge(lo_ready, H * b + s + 1)
                if later(b) or 2 * s + i // 2 > 0:
                    pe.wait_ge(pt_free[i % 2], 2 * (H * b + s) + i // 2)
                n = i + 1
                for part in range(2):
                    for k in range(n):
                        mm = pe.transpose(pt_bank[i % 2][:, (part * n + k) * P:(part * n + k + 1) * P],
                                          probs16[:, s % 2, part, OFF[i] + k * P:OFF[i] + (k + 1) * P],
                                          ident16[:])
                mm.then_inc(pt_full, 1)

            def weigh_values(b, s, i):
                if i == 0:
                    if later(b) or s >= 2:
                        pe.wait_ge(av_read, H * b + s - 1)
                    if s == 0:
                        pe.wait_ge(v_done, QT * b + QT)
                bank = av_bank[s % 2]
                pe.wait_ge(pt_free[i % 2], 2 * (H * b + s) + i // 2 + 1)
                n = i + 1
                for k in range(n):
                    at = 2 * OFF[i] + k * P
                    pe.matmul(bank[:, i * 96:(i + 1) * 96], probs_t[:, s % 2, at:at + P],
                              v_parts[:, k, s, :, :], start=(k == 0), stop=False)
                    at += n * P
                    mm = pe.matmul(bank[:, i * 96:i * 96 + 64], probs_t[:, s % 2, at:at + P],
                                   v_parts[:, k, s, 0:2, :], start=False, stop=(k == n - 1))
                if i == QT - 1:
                    mm.then_inc(av_full, 1)

            def turn_ctx(b, q):
                bank, used = pj_use(("c", q), b)
                pe.wait_ge(pj_free[bank], used)
                if q == 0:
                    pe.wait_ge(ctx_ready, H * b + H)
                for c in range(KC):
                    mm = pe.transpose(pj_bank[bank][:, c * P:(c + 1) * P], ctx_sb[:, q, c * P:(c + 1) * P],
                                      ident[:])
                mm.then_inc(pj_full, 1)

            def project_out(b, q):
                bank, used = pj_use(("o", q), b)
                pe.wait_ge(pj_free[bank], used)
                c_bank, c_used = pj_use(("c", q), b)
                if c_bank != bank:
                    pe.wait_ge(pj_free[c_bank], c_used + 1)
                e = 2 * (q % 2)
                product(pj_bank[bank], [(parts[:, e, c * P:(c + 1) * P], parts[:, e + 1, c * P:(c + 1) * P],
                                         w_hi[:, 3, c, :], w_lo[:, 3, c, :]) for c in range(KC)], (0, 1, 2, 3))

            def finish(b):
                if not later(b):
                    pe.wait_ge(wl_pool, 4)
                for kind, q in BACK:
                    (turn_ctx if kind == "c" else project_out)(b, q)

            def step(b, s, following):
                own, turned, weighed = back(b, s, 0), back(b, s, 2), back(b, s, 3)
                chunk = s // HPC + 1
                own_qk = s % HPC < 2 and chunk < KC and s < H
                for i in range(2):
                    if own:
                        scores(b, s, i)
                for i in range(2):
                    if weighed:
                        weigh_values(*weighed, i)
                if own_qk:
                    project_qk(b, "qk"[s % HPC], chunk, (0, 1))
                for i in range(2, QT):
                    if own:
                        scores(b, s, i)
                    if weighed:
                        weigh_values(*weighed, i)
                for i in range(2):
                    if turned:
                        turn_probs(*turned, i)
                if own_qk:
                    project_qk(b, "qk"[s % HPC], chunk, (2, 3))
                if following is not None and s == 10:
                    turn_x(following, 0)
                    turn_x(following, 1)
                if following is not None and s == 11:
                    turn_x(following, 2)
                    turn_x(following, 3)
                if following is not None and s in (12, 13):
                    project_qk(following, "qk"[s - 12], 0)
                for i in range(2, QT):
                    if turned:
                        turn_probs(*turned, i)
                if following is not None and s in (13, 14, 15):
                    for t in {13: (0,), 14: (1, 2), 15: (3,)}[s]:
                        project_v(following, t)

            for t in range(QT):
                turn_x(0, t)
            project_qk(0, "q", 0)
            project_qk(0, "k", 0)
            for t in range(QT):
                project_v(0, t)
            for s in range(HALF):
                step(0, s, None)
            with pe.Fori(1, B) as b:
                for s in range(HALF, H):
                    step(b - 1, s, b)
                for s in range(HALF):
                    step(b, s, None)
                    if s == 2:
                        finish(b - 1)
            for s in range(HALF, H + 3):
                step(B - 1, s, None)
            finish(B - 1)

        @block.vector
        def _(dve):
            def norm_stats(b, tiles):
                for t in tiles:
                    dve.wait_ge(x_ld[t % 2], 32 * b + 16 * (t // 2 + 1))
                    dve.bn_stats(stats[:, t, :], x_in[:, t % 2, :]).then_inc(ln_stats, 1)
                dve.wait_ge(ln_stats, QT * b + tiles[-1] + 1)
                dve.nop(nofuse=True)
                for t in tiles:
                    dve.bn_aggr(meanvar[:, t, :], stats[:, t, :]).then_inc(ln_mv, 1)
                dve.wait_ge(ln_mv, QT * b + tiles[-1] + 1)
                two = slice(tiles[0], tiles[-1] + 1)
                dve.tensor_scalar(varp[:, two], meanvar[:, two, 1], EPS, None, ALU.add).then_inc(ln_var, 1)

            def norm_apply(b, t):
                if t % 2 == 0:
                    dve.wait_ge(rstd_ready, 2 * b + t // 2 + 1)
                if t >= 2:
                    dve.wait_ge(pj_full, pj_total(("x", t - 2), b))
                dve.tensor_scalar(xn[:, t % 2, :], x_in[:, t % 2, :], meanvar[:, t, 0:1], rstd[:, t:t + 1],
                                  ALU.subtract, ALU.mult).then_inc(xn_ready, 1)

            def x_low(b, t):
                bank, _ = pj_use(("x", t), b)
                rows = slice(t * P, (t + 1) * P)
                dve.wait_ge(xh_ready, QT * b + t + 1)
                if later(b) and t == 0:
                    dve.wait_ge(xt_st, 32 * b)
                dve.tensor_tensor(xt_lo[:, :, rows], pj_bank[bank][:, :].rearrange("p (c n) -> p c n", c=KC),
                                  xt_hi[:, :, rows].bitcast(F32), ALU.subtract).then_inc(pj_free[bank], 1)

            def v_take(b, t):
                bank, _ = pj_use(("v", t), b)
                dve.wait_ge(pj_full, pj_total(("v", t), b))
                if later(b) and t == 0:
                    dve.wait_ge(v_done, QT * b)
                dve.tensor_tensor(v_full[:, t, :], pj_bank[bank][:, :], bv_all[:], ALU.add
                                  ).then_inc(pj_free[bank], 1)

            def v_split(b, t):
                full = v_full[:, t, :].rearrange("p (h d) -> p h d", h=H)
                dve.wait_ge(vh_ready, QT * b + t + 1)
                dve.tensor_tensor(full, full, v_parts[:, t, :, 0, :], ALU.subtract).then_inc(v_rest, 1)
                dve.wait_ge(v_rest, QT * b + t + 1)
                dve.tensor_copy(v_parts[:, t, :, 1, :], full).then_inc(v_mid, 1)
                dve.wait_ge(v_mid, QT * b + t + 1)
                dve.tensor_tensor(v_parts[:, t, :, 2, :], full, v_parts[:, t, :, 1, :],
                                  ALU.subtract).then_inc(v_done, 1)

            def bias_and_max(b, s):
                c, h = divmod(s, HPC)
                if later(b) or s >= 2:
                    dve.wait_ge(lo_ready, H * b + s - 1)
                for i in range(QT):
                    n = (i + 1) * P
                    dve.wait_ge(s_full, 64 * b + 4 * s + i + 1)
                    dve.nop(nofuse=True)
                    dve.tensor_tensor_reduce(
                        probs[:, s % 2, OFF[i]:OFF[i] + n], score_bank[i % 2][:, 0:n], dist4[:, h, S - n:S],
                        1.0, -3.4e38, ALU.add, ALU.max, row_max[:, s % 2, i:i + 1]).then_inc(t_done, 1)
                dve.wait_ge(t_done, 64 * b + 4 * s + 4)
                dve.tensor_scalar(neg_max[:, s % 2, :], row_max[:, s % 2, :], -(4.0**-c), None,
                                  ALU.mult).then_inc(nm_ready, 1)

            def probs_high(b, s):
                dve.wait_ge(p_ready, H * b + s + 1)
                if later(b) or s >= 2:
                    dve.wait_ge(pt_full, 4 * (H * b + s - 1))
                dve.tensor_copy(probs16[:, s % 2, 0, :], probs[:, s % 2, :]).then_inc(hi_ready, 1)

            def take_turned(b, s, i):
                n = 2 * (i + 1) * P
                dve.wait_ge(pt_full, 4 * (H * b + s) + i + 1)
                if later(b) or s >= 2:
                    dve.wait_ge(av_full, H * b + s - 1)
                dve.tensor_copy(probs_t[:, s % 2, 2 * OFF[i]:2 * OFF[i] + n],
                                pt_bank[i % 2][:, 0:n]).then_inc(pt_free[i % 2], 1)

            def normalize(b, s):
                dve.wait_ge(av_full, H * b + s + 1)
                if later(b) or s >= 2:
                    dve.wait_ge(ctx_ready, H * b + s - 1)
                dve.reciprocal(inv_sum[:, s % 2, :], row_sum[:, s % 4, :])
                dve.tensor_reduce(ctx_tmp[:, s % 2],
                                  av_bank[s % 2][:, 0:QT * 96].rearrange("p (q t d) -> p q d t", q=QT, t=3),
                                  AX_X, ALU.add).then_inc(av_read, 1)
                dve.wait_ge(av_read, H * b + s + 1)
                if s == 0:
                    if later(b):
                        dve.wait_ge(pj_full, pj_total(("c", QT - 1), b - 1))
                    else:
                        dve.wait_ge(coef_st, 16 * 2 * ROLES * MATS)
                dve.tensor_tensor(ctx_sb[:, :, s * HD:(s + 1) * HD], ctx_tmp[:, s % 2],
                                  inv_sum[:, s % 2, :].unsqueeze(2).broadcast_to([P, QT, HD]),
                                  ALU.mult).then_inc(ctx_ready, 1)

            def ctx_low(b, q):
                bank, _ = pj_use(("c", q), b)
                e = 2 * (q % 2)
                dve.wait_ge(ch_ready, QT * b + q + 1)
                dve.tensor_tensor(parts[:, e + 1, :], pj_bank[bank][:, :], parts[:, e, :].bitcast(F32),
                                  ALU.subtract).then_inc(pj_free[bank], 1)

            def add_residual(b, q):
                bank, _ = pj_use(("o", q), b)
                dve.wait_ge(pj_full, pj_total(("o", q), b))
                dve.wait_ge(res_ld[q % 2], 32 * b + 16 * (q // 2 + 1))
                dve.tensor_tensor(resid[:, q % 2, :], pj_bank[bank][:, :], resid[:, q % 2, :], ALU.add
                                  ).then_inc(pj_free[bank], 1)

            def finish(b, following):
                for n, (kind, q) in enumerate(BACK):
                    (ctx_low if kind == "c" else add_residual)(b, q)
                    if following is not None and n < QT:
                        v_split(following, n)

            def step(b, s, following):
                halved, turned, weighed = back(b, s, 1), back(b, s, 2), back(b, s, 3)
                if halved:
                    probs_high(*halved)
                if s < H:
                    bias_and_max(b, s)
                if turned:
                    take_turned(*turned, 0)
                    take_turned(*turned, 1)
                if weighed:
                    normalize(*weighed)
                if following is not None and s == 8:
                    norm_stats(following, (0, 1))
                if following is not None and s == 9:
                    norm_apply(following, 0)
                    norm_apply(following, 1)
                if following is not None and s == 10:
                    norm_stats(following, (2, 3))
                    x_low(following, 0)
                    norm_apply(following, 2)
                    x_low(following, 1)
                    norm_apply(following, 3)
                if following is not None and s == 11:
                    x_low(following, 2)
                    x_low(following, 3)
                if following is not None and s in (13, 14, 15):
                    for t in {13: (0,), 14: (1, 2), 15: (3,)}[s]:
                        v_take(following, t)

            def w_low(n):
                dve.wait_ge(wh_ready, n + 1)
                dve.tensor_tensor(w_piece(w_lo, n), w_raw[:, n % 3], w_piece(w_hi, n).bitcast(F32),
                                  ALU.subtract).then_inc(wl_ready, 1)

            def polynomials():
                steps = [0]

                def then(ins):
                    steps[0] += 1
                    ins.then_inc(poly_step, 1)
                    dve.wait_ge(poly_step, steps[0])

                p0, p1, p2, p3 = [points[:, k:k + 2, :] for k in range(4)]
                c1, c2, u, v = [tmp[:, k] for k in range(4)]
                a0, a1, a2, a3 = [poly[:, d] for d in range(4)]
                dve.wait_ge(points_ld, 32)
                dve.tensor_tensor(c1, p2, p0, ALU.subtract)
                dve.tensor_tensor(u, p3, p0, ALU.subtract)
                then(dve.tensor_tensor(v, p1, p2, ALU.subtract))
                dve.scalar_tensor_tensor(a3, v, 3.0, u, ALU.mult, ALU.add)
                then(dve.scalar_tensor_tensor(c2, p0, 2.0, p3, ALU.mult, ALU.subtract))
                then(dve.scalar_tensor_tensor(c2, p1, -5.0, c2, ALU.mult, ALU.add))
                dve.tensor_tensor(v, a3, phase, ALU.mult)
                then(dve.scalar_tensor_tensor(c2, p2, 4.0, c2, ALU.mult, ALU.add))
                then(dve.tensor_tensor(a2, v, c2, ALU.add))
                then(dve.tensor_tensor(a1, a2, phase, ALU.mult))
                then(dve.tensor_tensor(a1, a1, c1, ALU.add))
                then(dve.tensor_tensor(a0, a1, phase, ALU.mult))
                dve.scalar_tensor_tensor(a0, p1, 2.0, a0, ALU.mult, ALU.add)
                then(dve.tensor_tensor(a2, a2, v, ALU.add))
                then(dve.tensor_tensor(u, a2, phase, ALU.mult))
                dve.tensor_tensor(a2, a2, v, ALU.add)
                then(dve.tensor_tensor(a1, a1, u, ALU.add))

            dve.memset(minus_half[:], -0.5).then_inc(small_set, 1)
            norm_stats(0, (0, 1))
            w_low(0)
            norm_apply(0, 0)
            norm_apply(0, 1)
            w_low(1)
            x_low(0, 0)
            x_low(0, 1)
            norm_stats(0, (2, 3))
            dve.wait_ge(const_ld, 16 * 6)
            dve.tensor_copy(ident16[:], ident[:]).then_inc(small_set, 1)
            for c in range(KC):
                dve.tensor_scalar(b_scaled[:, c:c + 1], b_qk[:, 0, c:c + 1], float(HD) ** -0.5 * 4.0**c, None,
                                  ALU.mult).then_inc(small_set, 1)
            norm_apply(0, 2)
            norm_apply(0, 3)
            x_low(0, 2)
            x_low(0, 3)
            w_low(2)
            w_low(3)
            polynomials()
            for t in range(QT):
                v_take(0, t)
            for h in range(HPC):
                dve.tensor_scalar(dist4[:, h], dist4[:, HPC - 1] if h < HPC - 1 else dist4[:, h],
                                  2.0 ** (-8.0 / H * (h + 1)), None, ALU.mult).then_inc(small_set, 1)
            for t in range(QT):
                v_split(0, t)
            dve.wait_ge(ph_ready, 1)
            dve.tensor_tensor(poly_lo.rearrange("p d e m n -> p (d e m n)"),
                              poly.rearrange("p d e n -> p (d e n)"),
                              poly_hi.rearrange("p d e m n -> p (d e m n)").bitcast(F32),
                              ALU.subtract).then_inc(pl_ready, 1)
            dve.wait_ge(wl_pool, 4)
            dve.wait_ge(wl_ready, 4)
            dve.wait_ge(pl_ready, 1)
            dve.wait_ge(small_set, 2 + KC + HPC)
            for s in range(HALF):
                step(0, s, None)
            with dve.Fori(1, B) as b:
                for s in range(HALF, H):
                    step(b - 1, s, b)
                for s in range(HALF):
                    step(b, s, None)
                    if s == 2:
                        finish(b - 1, b)
            for s in range(HALF, H + 3):
                step(B - 1, s, None)
            finish(B - 1, None)

        @block.scalar
        def _(act):
            def x_high(b, t):
                bank, _ = pj_use(("x", t), b)
                act.wait_ge(pj_full, pj_total(("x", t), b))
                if later(b) and t == 0:
                    act.wait_ge(xt_st, 32 * b)
                act.copy(xt_hi[:, :, t * P:(t + 1) * P],
                         pj_bank[bank][:, :].rearrange("p (c n) -> p c n", c=KC)).then_inc(xh_ready, 1)

            def qk_high(b, name, c):
                m = "qk".index(name)
                bank, _ = pj_use((name, c), b)
                scale = float(HD) ** -0.5 * 4.0**c if m == 0 else 1.0
                bias = b_scaled[:, c:c + 1] if m == 0 else b_qk[:, 1, c:c + 1]
                act.wait_ge(pj_full, pj_total((name, c), b))
                if later(b) or c > 0:
                    act.wait_ge(ql_ready, 8 * b + 2 * c + m - 1)
                act.activation(qk_full[:, m, :], pj_bank[bank][:, :], ACT.Identity, bias=bias,
                               scale=scale).then_inc(full_ready, 1)
                if c > 0:
                    act.wait_ge(stacked[(c - 1) % 2], 2 * STACK * b + STACK * ((c - 1) // 2 + 1))
                act.activation(parts[:, 2 * m, :], pj_bank[bank][:, :], ACT.Identity, bias=bias,
                               scale=scale).then_inc(pj_free[bank], 1)

            def v_high(b, t):
                bank, used = pj_use(("v", t), b)
                act.wait_ge(pj_free[bank], used + 1)
                if later(b) and t == 0:
                    act.wait_ge(av_full, H * b)
                act.copy(v_parts[:, t, :, 0, :],
                         v_full[:, t, :].rearrange("p (h d) -> p h d", h=H)).then_inc(vh_ready, 1)

            def exponentials(b, s):
                act.wait_ge(nm_ready, H * b + s + 1)
                if later(b) or s >= 4:
                    act.wait_ge(av_read, H * b + s - 3)
                for i in range(QT):
                    tile = probs[:, s % 2, OFF[i]:OFF[i] + (i + 1) * P]
                    e = act.activation(tile, tile, ACT.Exp, bias=neg_max[:, s % 2, i:i + 1],
                                       scale=4.0**-(s // HPC), accum_out=row_sum[:, s % 4, i:i + 1])
                e.then_inc(p_ready, 1)

            def take_turned(b, s, i):
                n = 2 * (i + 1) * P
                act.wait_ge(pt_full, 4 * (H * b + s) + i + 1)
                if later(b) or s >= 2:
                    act.wait_ge(av_full, H * b + s - 1)
                act.copy(probs_t[:, s % 2, 2 * OFF[i]:2 * OFF[i] + n],
                         pt_bank[i % 2][:, 0:n]).then_inc(pt_free[i % 2], 1)

            def ctx_high(b, q):
                bank, _ = pj_use(("c", q), b)
                act.wait_ge(pj_full, pj_total(("c", q), b))
                act.copy(parts[:, 2 * (q % 2), :], pj_bank[bank][:, :]).then_inc(ch_ready, 1)

            def finish(b, following):
                if following is not None:
                    act.wait_ge(stacked[1], 2 * STACK * following + STACK)
                for q in range(QT):
                    if following is not None:
                        v_high(following, q)
                    ctx_high(b, q)

            def step(b, s, following):
                turned = back(b, s, 2)
                chunk = s // HPC + 1
                if s < H:
                    exponentials(b, s)
                if s % HPC < 2 and chunk < KC and s < H:
                    qk_high(b, "qk"[s % HPC], chunk)
                if following is not None and s in (10, 11):
                    x_high(following, 2 * (s - 10))
                    x_high(following, 2 * (s - 10) + 1)
                if following is not None and s in (12, 13):
                    qk_high(following, "qk"[s - 12], 0)
                if turned:
                    take_turned(*turned, 2)
                    take_turned(*turned, 3)

            def w_high(n):
                act.wait_ge(w_ld[n % 3], 16 * (n // 3 + 1))
                act.copy(w_piece(w_hi, n), w_raw[:, n % 3]).then_inc(wh_ready, 1)

            act.dma_start(ident[:], c_ident).then_inc(const_ld, 16)
            act.dma_start(b_qk[:, 0, :], bq).then_inc(const_ld, 16)
            act.dma_start(b_qk[:, 1, :], bk).then_inc(const_ld, 16)
            act.dma_start(bv_all[:], bv.partition_broadcast(P)).then_inc(const_ld, 16)
            act.dma_start(basis_raw, c_basis).then_inc(const_ld, 16)
            act.dma_start(dist4[:, HPC - 1, :], c_dist).then_inc(const_ld, 16)
            act.dma_start(points, win).then_inc(points_ld, 16)
            act.dma_start(phase, c_phase).then_inc(points_ld, 16)
            w_high(0)
            w_high(1)
            x_high(0, 0)
            x_high(0, 1)
            w_high(2)
            x_high(0, 2)
            x_high(0, 3)
            w_high(3)
            act.wait_ge(small_set, 2 + KC)
            qk_high(0, "q", 0)
            w_high(4)
            w_high(5)
            qk_high(0, "k", 0)
            act.copy(basis[:], basis_raw)
            for n in range(6, W_PIECES):
                w_high(n)
            act.wait_ge(poly_step, 11)
            act.copy(poly_hi.rearrange("p d e m n -> p (d e m n)"),
                     poly.rearrange("p d e n -> p (d e n)")).then_inc(ph_ready, 1)
            for t in range(QT):
                v_high(0, t)
            for s in range(HALF):
                step(0, s, None)
            with act.Fori(1, B) as b:
                for s in range(HALF, H):
                    step(b - 1, s, b)
                for s in range(HALF):
                    step(b, s, None)
                    if s == 2:
                        finish(b - 1, b)
            for s in range(HALF, H + 3):
                step(B - 1, s, None)
            finish(B - 1, None)

        @block.gpsimd
        def _(pool):
            def inverse_std(b, n):
                two = slice(2 * n, 2 * n + 2)
                pool.wait_ge(ln_var, 2 * b + n + 1)
                pool.tensor_tensor(rstd[:, two], varp[:, two], minus_half[:, two], ALU.pow
                                   ).then_inc(rstd_ready, 1)

            def qk_low(b, name, c):
                m = "qk".index(name)
                bank, used = pj_use((name, c), b)
                pool.wait_ge(pj_free[bank], used + 1)
                pool.tensor_tensor(parts[:, 2 * m + 1, :], qk_full[:, m, :], parts[:, 2 * m, :].bitcast(F32),
                                   ALU.subtract).then_inc(ql_ready, 1)

            def probs_low(b, s):
                pool.wait_ge(hi_ready, H * b + s + 1)
                pool.tensor_tensor(probs16[:, s % 2, 1, :], probs[:, s % 2, :], probs16[:, s % 2, 0, :],
                                   ALU.subtract).then_inc(lo_ready, 1)

            def step(b, s, following):
                halved = back(b, s, 1)
                chunk = s // HPC + 1
                if halved:
                    probs_low(*halved)
                if s % HPC < 2 and chunk < KC and s < H:
                    qk_low(b, "qk"[s % HPC], chunk)
                if following is not None and s in (8, 10):
                    inverse_std(following, (s - 8) // 2)
                if following is not None and s in (12, 13):
                    qk_low(following, "qk"[s - 12], 0)

            pool.wait_ge(small_set, 1)
            inverse_std(0, 0)
            inverse_std(0, 1)
            for n in range(4, 6):
                pool.wait_ge(wh_ready, n + 1)
                pool.tensor_tensor(w_piece(w_lo, n), w_raw[:, n % 3], w_piece(w_hi, n).bitcast(F32),
                                   ALU.subtract).then_inc(wl_pool, 1)
            qk_low(0, "q", 0)
            qk_low(0, "k", 0)
            for n in range(6, W_PIECES):
                pool.wait_ge(wh_ready, n + 1)
                pool.tensor_tensor(w_piece(w_lo, n), w_raw[:, n % 3], w_piece(w_hi, n).bitcast(F32),
                                   ALU.subtract).then_inc(wl_pool, 1)
            for s in range(HALF):
                step(0, s, None)
            with pool.Fori(1, B) as b:
                for s in range(HALF, H):
                    step(b - 1, s, b)
                for s in range(HALF):
                    step(b, s, None)
            for s in range(HALF, H + 1):
                step(B - 1, s, None)

        @block.sync
        def _(sp):
            def load_x(b, t):
                if t >= 2:
                    sp.wait_ge(xn_ready, QT * b + t - 1)
                    sp.nop(nofuse=True)
                sp.dma_start(x_in[:, t % 2, :], rows_of(x_t, QT * b + t)).then_inc(x_ld[t % 2], 16)

            def store_xt(b):
                for t in range(QT - 2, QT):
                    bank, used = pj_use(("x", t), b)
                    sp.wait_ge(pj_free[bank], used + 1)
                    sp.nop(nofuse=True)
                for e, part in enumerate((xt_hi, xt_lo)):
                    sp.dma_start(rows_of(xt_d, 2 * b + e), part[:].rearrange("p c n -> p (c n)").bitcast(F32)
                                 ).then_inc(xt_st, 16)

            def stack(b, c):
                if later(b) or c >= 2:
                    sp.wait_ge(s_full, 64 * b + 16 * (c - 1))
                    sp.nop(nofuse=True)
                for m, stacks in ((0, q_stack), (1, k_stack)):
                    sp.wait_ge(ql_ready, 8 * b + 2 * c + m + 1)
                    sp.nop(nofuse=True)
                    for role, low in enumerate(((0, 1, 0), (0, 0, 1))[m]):
                        sp.dma_start(
                            stacks[role * HD:(role + 1) * HD, c % 2].rearrange("d h n -> d (h n)").bitcast(F32),
                            parts[:, 2 * m + low, :].bitcast(F32)).then_inc(stacked[c % 2], 16)

            def load_residual(b, q):
                if later(b) or q >= 2:
                    sp.wait_ge(res_st[q % 2], 32 * b + 16 * (q // 2))
                    sp.nop(nofuse=True)
                sp.dma_start(resid[:, q % 2, :], rows_of(x_t, QT * b + q)).then_inc(res_ld[q % 2], 16)

            def store_sum(b, q):
                bank, used = pj_use(("o", q), b)
                sp.wait_ge(pj_free[bank], used + 1)
                sp.nop(nofuse=True)
                sp.dma_start(rows_of(mid_d, QT * b + q), resid[:, q % 2, :]).then_inc(res_st[q % 2], 16)

            def finish(b):
                for q in range(2):
                    store_sum(b, q)
                    load_residual(b, q + 2)
                for q in range(2, QT):
                    store_sum(b, q)

            def load_piece(n):
                m, half = divmod(n, 2)
                if n >= 7:
                    sp.wait_ge(wl_pool, n - 6)
                elif n >= 3:
                    sp.wait_ge(wl_ready, n - 2)
                src = weights[m].rearrange("(c p) n -> p c n", p=P)
                sp.dma_start(w_raw[:, n % 3], src[:, 2 * half:2 * half + 2, :]).then_inc(w_ld[n % 3], 16)

            load_x(0, 0)
            load_x(0, 1)
            for n in range(3):
                load_piece(n)
            load_x(0, 2)
            load_x(0, 3)
            for n in range(3, W_PIECES):
                load_piece(n)
            store_xt(0)
            stack(0, 0)
            sp.wait_ge(pl_ready, 1)
            for e in range(2):
                for role, part in enumerate((poly_hi, poly_hi, poly_lo)):
                    for m in range(MATS):
                        sp.dma_start(
                            coef_d[e, 4 * role:4 * role + 4, m, :].rearrange("d (p n) -> p d n", p=P),
                            part[:, :, e, m, :].bitcast(F32)).then_inc(coef_st, 16)
            stack(0, 1)
            sp.wait_ge(coef_st, 16 * 2 * ROLES * MATS)
            load_residual(0, 0)
            load_residual(0, 1)
            stack(0, 2)
            with sp.Fori(1, B) as b:
                for t in range(QT):
                    load_x(b, t)
                stack(b - 1, 3)
                store_xt(b)
                stack(b, 0)
                stack(b, 1)
                finish(b - 1)
                load_residual(b, 0)
                load_residual(b, 1)
                stack(b, 2)
            stack(B - 1, 3)
            finish(B - 1)
            for q in range(2):
                sp.wait_ge(res_st[q], 32 * B)
            sp.wait_ge(xt_st, 32 * B)


def ffn(nc, sems, psum, basis, c_mask, coef_d, xt_d, mid_d, bo, out_t):
    NT = B * QT
    with ExitStack() as ctx:
        sb = lambda n, s, dt: ctx.enter_context(nc.sbuf_tensor(n, s, dt))
        xt = sb("xt", [P, B, 2, KC, S], F32R)
        acc = sb("acc", [P, NT, D], F32)
        w_hi = sb("fw_hi", [P, 2, MATS, PW], F32R)
        w_lo = sb("fw_lo", [P, 2, MATS, PW], F32R)
        in_hi = sb("in_hi", [P, 2, 2, S], F32R)
        in_lo = sb("in_lo", [P, 2, 2, S], F32R)
        silu = sb("silu", [P, 2, S], F32)
        inner = sb("inner", [P, 2, S], F32)
        w_new = sb("w_new", [P, 2, 512], F32)
        coef = sb("coef", [END_ROW + KPOLY, 2, MATS, PW], F32R)
        mask = sb("mask", [P, 2, 2, PW], U8)
        bo_all = sb("bo_all", [P, D], F32)

        gate_bank, up_bank, down_bank = psum[0:2], psum[2:4], psum[4:6]
        start_bank, end_bank = psum[6], psum[7]
        def last(pair):
            return isinstance(pair, int) and pair == PAIRS - 1

        GROUPS = MATS * 2

        xt_ld = sems(ctx, *[f"xt_ld{b}" for b in range(B)])
        acc_ld = sems(ctx, *[f"acc_ld{b}" for b in range(B)])
        coef_ld = [sems(ctx, *[f"coef_ld{sl}_{m}" for m in range(MATS)]) for sl in range(2)]
        mask_ld = sems(ctx, "mask_ld0", "mask_ld1")
        (bo_ld, bo_added, ends_full, start_read, w_merged, wh_ready, wl_ready, gate_full, up_full, silu_ready,
         inner_ready, ih_ready, il_ready, down_full, down_added, stored) = sems(
            ctx, "bo_ld", "bo_added", "ends_full", "start_read", "w_merged", "wh_ready", "wl_ready", "gate_full",
            "up_full", "silu_ready", "inner_ready", "ih_ready", "il_ready", "down_full", "down_added", "stored")

        block = ctx.enter_context(nc.Block())

        WGEN = {0: (0, 1), 1: (2, 3), 2: (4, 5), 3: ()}

        @block.tensor
        def _(pe):
            def make(pair, g, sl):
                m, half = divmod(g, 2)
                cols = slice(half * 512, (half + 1) * 512)
                if half == 0:
                    pe.wait_ge(coef_ld[sl][m], 16 * pair + 32 - 16 * sl)
                if later(pair) or g:
                    pe.wait_ge(w_merged, GROUPS * pair + g)
                pe.matmul(start_bank[:, :], basis[0:KPOLY, :], coef[0:KPOLY, sl, m, cols], start=True, stop=True)
                pe.matmul(end_bank[:, :], basis[END_ROW:END_ROW + KPOLY, :],
                          coef[END_ROW:END_ROW + KPOLY, sl, m, cols], start=True, stop=True).then_inc(ends_full, 1)

            def gate_or_up(m, pair, sl, t, j):
                k = 4 * pair + t
                if j == 0 and m == 0 and not later(pair):
                    pe.wait_ge(xt_ld[t], 16)
                if t == 0 and j == 0:
                    pe.wait_ge(wl_ready, GROUPS * pair + 2 * (m + 1))
                bank, full = ((gate_bank, gate_full), (up_bank, up_full))[m]
                if later(k):
                    pe.wait_ge((silu_ready, inner_ready)[m], 2 * k + j - 1)
                for q in range(KC):
                    cols = slice(q * 2 * P + j * P, q * 2 * P + (j + 1) * P)
                    hi, lo = w_hi[:, sl, m, cols], w_lo[:, sl, m, cols]
                    pe.matmul(bank[j][:, :], hi, xt[:, t, 0, q, :], start=(q == 0), stop=False)
                    pe.matmul(bank[j][:, :], hi, xt[:, t, 1, q, :], start=False, stop=False)
                    mm = pe.matmul(bank[j][:, :], lo, xt[:, t, 0, q, :], start=False, stop=(q == KC - 1))
                mm.then_inc(full, 1)

            def down(pair, sl, t):
                k = 4 * pair + t
                pe.wait_ge(il_ready, 2 * k + 2)
                if t == 0:
                    pe.wait_ge(wl_ready, GROUPS * pair + GROUPS)
                for i in range(QT):
                    bank = down_bank[i % 2]
                    if later(k) or i >= 2:
                        pe.wait_ge(down_added, QT * k + i - 1)
                    for j in range(2):
                        hi, lo = in_hi[:, t % 2, j, i * P:(i + 1) * P], in_lo[:, t % 2, j, i * P:(i + 1) * P]
                        r_hi, r_lo = [w[:, sl, 2, j * 512:(j + 1) * 512] for w in (w_hi, w_lo)]
                        pe.matmul(bank[:, :], hi, r_hi, start=(j == 0), stop=False)
                        pe.matmul(bank[:, :], hi, r_lo, start=False, stop=False)
                        mm = pe.matmul(bank[:, :], lo, r_hi, start=False, stop=(j == 1))
                    mm.then_inc(down_full, 1)

            def body(it):
                for sl in range(2):
                    pair = 2 * it + sl
                    for t in range(B):
                        k = 4 * pair + t
                        made = WGEN[t] if not last(pair) else ()
                        for j in range(2):
                            gate_or_up(0, pair, sl, t, j)
                            if not later(k):
                                make(0, 2 + j, 0)
                        for j in range(2):
                            gate_or_up(1, pair, sl, t, j)
                            if not later(k):
                                make(0, 4 + j, 0)
                        for g in made[:1]:
                            make(pair + 1, g, 1 - sl)
                        if t:
                            down(pair, sl, t - 1)
                        elif later(k):
                            down(pair - 1, 1 - sl, B - 1)
                        for g in made[1:]:
                            make(pair + 1, g, 1 - sl)

            make(0, 0, 0)
            make(0, 1, 0)
            body(0)
            with pe.Fori(1, PAIRS // 2 - 1) as it:
                body(it)
            body(PAIRS // 2 - 1)
            down(PAIRS - 1, 1, B - 1)

        @block.scalar
        def _(act):
            def start_part(pair, g):
                act.wait_ge(ends_full, GROUPS * pair + g + 1)
                if later(pair) or g >= 2:
                    act.wait_ge(wl_ready, GROUPS * pair + g - 1)
                act.copy(w_new[:, g % 2, :], start_bank[:, :]).then_inc(start_read, 1)

            def high(pair, g, sl):
                m, half = divmod(g, 2)
                act.wait_ge(w_merged, GROUPS * pair + g + 1)
                act.copy(w_hi[:, sl, m, half * 512:(half + 1) * 512], w_new[:, g % 2, :]).then_inc(wh_ready, 1)

            def gated(k, t, j):
                act.wait_ge(gate_full, 2 * k + j + 1)
                if later(k):
                    act.wait_ge(inner_ready, 2 * k + j - 1)
                act.activation(silu[:, j, :], gate_bank[j][:, :], ACT.Silu).then_inc(silu_ready, 1)

            def inner_high(k, t, j):
                act.wait_ge(inner_ready, 2 * k + j + 1)
                if not isinstance(k, int) or k >= 2:
                    act.wait_ge(down_full, QT * (k - 1))
                act.copy(in_hi[:, t % 2, j, :], inner[:, j, :]).then_inc(ih_ready, 1)

            def body(it):
                for sl in range(2):
                    pair = 2 * it + sl
                    for t in range(B):
                        k = 4 * pair + t
                        made = WGEN[t] if not last(pair) else ()
                        for j in range(2):
                            gated(k, t, j)
                            if not later(k):
                                start_part(0, 2 + j)
                                high(0, 2 + j, 0)
                        for j in range(2):
                            inner_high(k, t, j)
                            if not later(k):
                                start_part(0, 4 + j)
                                high(0, 4 + j, 0)
                        for g in made:
                            start_part(pair + 1, g)
                            high(pair + 1, g, 1 - sl)

            for g in range(2):
                start_part(0, g)
                high(0, g, 0)
            body(0)
            with act.Fori(1, PAIRS // 2 - 1) as it:
                body(it)
            body(PAIRS // 2 - 1)

        @block.vector
        def _(dve):
            def merge(pair, g, sl):
                m, half = divmod(g, 2)
                if g == 0:
                    dve.wait_ge(mask_ld[sl], 8 * pair + 16 - 8 * sl)
                    dve.nop(nofuse=True)
                dve.wait_ge(start_read, GROUPS * pair + g + 1)
                dve.nop(nofuse=True)
                dve.copy_predicated(w_new[:, g % 2, :], mask[:, sl, m // 2, half * 512:(half + 1) * 512],
                                    end_bank[:, :]).then_inc(w_merged, 1)

            def low(pair, g, sl):
                m, half = divmod(g, 2)
                cols = slice(half * 512, (half + 1) * 512)
                dve.wait_ge(wh_ready, GROUPS * pair + g + 1)
                dve.tensor_tensor(w_lo[:, sl, m, cols], w_new[:, g % 2, :], w_hi[:, sl, m, cols].bitcast(F32),
                                  ALU.subtract).then_inc(wl_ready, 1)

            def multiply(k, t, j):
                dve.wait_ge(silu_ready, 2 * k + j + 1)
                dve.wait_ge(up_full, 2 * k + j + 1)
                if later(k):
                    dve.wait_ge(il_ready, 2 * k + j - 1)
                dve.tensor_tensor(inner[:, j, :], up_bank[j][:, :], silu[:, j, :], ALU.mult
                                  ).then_inc(inner_ready, 1)

            def add_down(pair, t, tiles):
                k = 4 * pair + t
                if not later(pair) and tiles[0] == 0:
                    dve.wait_ge(acc_ld[t], 16 * QT)
                    dve.wait_ge(bo_added, QT * (t + 1))
                for i in tiles:
                    at = acc[:, QT * t + i, :]
                    dve.wait_ge(down_full, QT * k + i + 1)
                    dve.tensor_tensor(at, down_bank[i % 2][:, :], at, ALU.add).then_inc(down_added, 1)

            def body(it):
                for sl in range(2):
                    pair = 2 * it + sl
                    for t in range(B):
                        k = 4 * pair + t
                        made = WGEN[t] if not last(pair) else ()
                        if not later(k):
                            for g in (2, 3):
                                merge(0, g, 0)
                                low(0, g, 0)
                        for j in range(2):
                            multiply(k, t, j)
                            if not later(k):
                                merge(0, 4 + j, 0)
                                low(0, 4 + j, 0)
                        done = (pair, t - 1) if t else (pair - 1, B - 1)
                        for g in made[:1]:
                            merge(pair + 1, g, 1 - sl)
                        if later(k):
                            add_down(*done, (0,))
                        for g in made[:1]:
                            low(pair + 1, g, 1 - sl)
                        if later(k):
                            add_down(*done, (1, 2, 3))
                        for g in made[1:]:
                            merge(pair + 1, g, 1 - sl)
                            low(pair + 1, g, 1 - sl)

            for g in range(2):
                merge(0, g, 0)
                low(0, g, 0)
            body(0)
            with dve.Fori(1, PAIRS // 2 - 1) as it:
                body(it)
            body(PAIRS // 2 - 1)
            add_down(PAIRS - 1, B - 1, range(QT))

        @block.gpsimd
        def _(pool):
            def inner_low(k, t, j):
                pool.wait_ge(ih_ready, 2 * k + j + 1)
                if not isinstance(k, int) or k >= 2:
                    pool.wait_ge(down_full, QT * (k - 1))
                pool.tensor_tensor(in_lo[:, t % 2, j, :], inner[:, j, :], in_hi[:, t % 2, j, :].bitcast(F32),
                                   ALU.subtract).then_inc(il_ready, 1)

            def body(it):
                for sl in range(2):
                    pair = 2 * it + sl
                    for t in range(B):
                        for j in range(2):
                            inner_low(4 * pair + t, t, j)
                        if isinstance(pair, int) and pair == 0:
                            pool.wait_ge(bo_ld, 16)
                            pool.wait_ge(acc_ld[t], 16 * QT)
                            for i in range(QT):
                                at = acc[:, QT * t + i, :]
                                pool.tensor_tensor(at, at, bo_all[:], ALU.add).then_inc(bo_added, 1)

            body(0)
            with pool.Fori(1, PAIRS // 2) as it:
                body(it)

        @block.sync
        def _(sp):
            def load_weights(pair, sl):
                at = pair * PW
                for m in range(MATS):
                    if later(pair - 1):
                        sp.wait_ge(ends_full, GROUPS * (pair - 2) + 2 * (m + 1))
                        sp.nop(nofuse=True)
                    for e, row in ((0, 0), (1, END_ROW)):
                        src = coef_d[e, :, m, at:at + PW] if isinstance(at, int) else \
                            coef_d[e, :, m, bass.ds(at, PW)]
                        sp.dma_start(coef[row:row + KPOLY, sl, m, :].bitcast(F32), src
                                     ).then_inc(coef_ld[sl][m], 16)
                if isinstance(pair, int):
                    src = c_mask[pair]
                else:
                    src = c_mask[bass.ds(pair, 1)].rearrange("a p k n -> (a p) k n")
                if later(pair - 1):
                    sp.wait_ge(w_merged, GROUPS * (pair - 1))
                    sp.nop(nofuse=True)
                sp.dma_start(mask[:, sl].bitcast(U32), src).then_inc(mask_ld[sl], 16)

            def body(it):
                for sl in range(2):
                    load_weights(2 * it + sl + 2, sl)

            load_weights(0, 0)
            for b in range(B):
                sp.dma_start(xt[:, b].rearrange("p e c n -> p e (c n)").bitcast(F32),
                             xt_d[2 * b:2 * b + 2].rearrange("e p n -> p e n")).then_inc(xt_ld[b], 16)
                if b == 0:
                    load_weights(1, 1)
            sp.dma_start(bo_all[:], bo.partition_broadcast(P)).then_inc(bo_ld, 16)
            for n in range(NT):
                sp.dma_start(acc[:, n, :], mid_d[n]).then_inc(acc_ld[n // QT], 16)
            body(0)
            with sp.Fori(1, PAIRS // 2 - 1) as it:
                body(it)
            for n in range(NT):
                sp.wait_ge(down_added, QT * B * (PAIRS - 1) + n + 1)
                sp.dma_start(out_t[n], acc[:, n, :]).then_inc(stored, 16)
            sp.wait_ge(stored, 16 * NT)


_INS = ["x", "Wq", "Wk", "Wv", "Wo", "bq", "bk", "bv", "bo"]


def kernel(**inputs):
    import concourse.bacc as _bacc
    from concourse.bass_utils import run_bass_kernel_spmd as _run

    nc = _bacc.Bacc("TRN2", target_bir_lowering=False, num_devices=1)
    arrays = {n: np.ascontiguousarray(inputs[f"L0_attn_{n}"]) for n in _INS}
    for n in ("Wq", "Wk", "bq", "bk"):
        w = arrays[n]
        arrays[n] = np.ascontiguousarray(w.reshape(-1, KC, HPC, HD).swapaxes(2, 3).reshape(w.shape))
    for n in ("bq", "bk"):
        arrays[n] = np.ascontiguousarray(arrays[n].reshape(KC, P).T)
    arrays["windows"] = control_windows([np.asarray(inputs[f"L0_ffn_{n}_cp"]) for n in ("gate", "up", "down")])
    arrays.update(shape_constants())
    order = [*_INS, "windows", "c_basis", "c_phase", "c_mask", "c_dist", "c_ident"]
    args = [nc.dram_tensor(n, arrays[n].shape, mybir.dt.from_np(arrays[n].dtype), kind="ExternalInput").ap()
            for n in order]
    result = nc.dram_tensor("result", (B, S, D), F32, kind="ExternalOutput").ap()
    build_kernel(nc, *args, result)
    r = _run(nc, [arrays], core_ids=[0])
    return r.results[0]["result"]
```

```python
from contextlib import ExitStack

import numpy as np

import concourse.bass as bass
from concourse import mybir

F32 = mybir.dt.float32
F32R = mybir.dt.float32r
F16 = mybir.dt.float16
BF16 = mybir.dt.bfloat16
U8 = mybir.dt.uint8
U32 = mybir.dt.uint32
ALU = mybir.AluOpType
ACT = mybir.ActivationFunctionType
AX_X = mybir.AxisListType.X

P = 128
B, S, D = 4, 512, 512
H, HD = 16, 32
INTER = 2048
KC = D // P
HPC = P // HD
QT = S // P
EPS = 1e-5
MASKED = -3.0e38
COMPRESSION = 128.9
N_CTRL = max(16, int(INTER * D / COMPRESSION))
MATS = 3
BLOCKS = INTER * D // P
PAIRS = INTER // (2 * P)
PW = BLOCKS // PAIRS
ROLES = 3
KPOLY = 4 * ROLES
END_ROW = 32

OFF = [0, 128, 384, 768]
PROBS = 1280


def grid():
    t = np.linspace(0.0, N_CTRL - 1.0, INTER * D, dtype=np.float64)
    seg = np.clip(np.floor(t).astype(np.int64), 0, N_CTRL - 2)
    return t, seg


def block_order():
    gate = [KC * (pr * 2 * P + i) + q for pr in range(PAIRS) for q in range(KC) for i in range(2 * P)]
    down = [(INTER // P) * o + 2 * pr + j for pr in range(PAIRS) for j in range(2) for o in range(D)]
    return np.array(gate), np.array(down)


def rounded(x):
    u = np.asarray(x, np.float32).view(np.uint32)
    return ((u + 0x7FF + ((u >> 12) & 1)) & np.uint32(0xFFFFF000)).view(np.float32)


def shape_constants():
    t, seg = grid()
    delta = (N_CTRL - 1.0) / (INTER * D - 1)
    basis = np.zeros((END_ROW + KPOLY, P), np.float32)
    for row, tau in ((0, np.arange(P) * delta), (END_ROW, (np.arange(P) - (P - 1)) * delta)):
        for d in range(4):
            hi = rounded(tau**d)
            lo = rounded(tau**d - hi)
            for role, part in enumerate((hi, lo, hi)):
                basis[row + 4 * role + d] = 0.5 * part
    phase = np.zeros((P, 2, MATS, BLOCKS // P), np.float32)
    mask = np.zeros((PAIRS, P, 2, PW), np.uint8)
    for kind, order in enumerate(block_order()):
        start, end = order * P, order * P + P - 1
        at = [t[start] - seg[start], t[end] - (seg[start] + 1)]
        for m in ((0, 1), (2,))[kind]:
            for e in range(2):
                phase[:, e, m, :] = at[e].reshape(P, -1)
        behind = seg.reshape(-1, P)[order] != seg[start][:, None]
        mask[:, :, kind, :] = behind.reshape(PAIRS, PW, P).transpose(0, 2, 1)
    key = np.arange(S)
    dist = np.broadcast_to((key - (S - 1)).astype(np.float32), (P, S)).copy()
    dist[(key[None, :] - (S - P)) > np.arange(P)[:, None]] = MASKED
    head = np.arange(P)[:, None] % HPC + HPC * np.arange(KC)
    scale = HD**-0.5 * 2.0 ** (8.0 / H * (head + 1))
    return {"c_basis": basis, "c_phase": phase, "c_mask": mask.view(np.uint32), "c_dist": dist,
            "c_ident": np.eye(P, dtype=np.float32), "c_scale": scale.astype(np.float32)}


def control_windows(points):
    _, seg = grid()
    out = []
    for order in block_order():
        first = seg[order * P]
        index = np.clip(first[None, :] + np.arange(-1, 4)[:, None], 0, N_CTRL - 1)
        out.append(index)
    rows = [points[m][out[0 if m < 2 else 1]] for m in range(MATS)]
    return np.ascontiguousarray(np.stack(rows).reshape(MATS, 5, P, -1).transpose(2, 1, 0, 3))


def later(b):
    return not isinstance(b, int) or b > 0


def rows_of(ap, index):
    if isinstance(index, int):
        return ap[index]
    return ap[bass.ds(index, 1)].rearrange("a p n -> (a p) n")


def build_kernel(nc, x, wq, wk, wv, wo, bq, bk, bv, bo, win, c_basis, c_phase, c_mask, c_dist, c_ident, c_scale, out):
    coef_d = nc.dram_tensor("coef_scratch", (2, KPOLY, MATS, BLOCKS), F32, kind="Internal").ap()
    xt_d = nc.dram_tensor("xt_scratch", (B * 2, P, KC * S), F32, kind="Internal").ap()
    mid_d = nc.dram_tensor("mid_scratch", (B * QT, P, D), F32, kind="Internal").ap()
    x_t = x.rearrange("b (t p) d -> (b t) p d", p=P)
    out_t = out.rearrange("b (t p) d -> (b t) p d", p=P)

    with ExitStack() as outer:
        def sems(ctx, *names):
            return [ctx.enter_context(nc.semaphore(n)) for n in names]

        psum = [outer.enter_context(nc.psum_tensor(f"bank{i}", [P, 512], F32)) for i in range(8)]
        basis = outer.enter_context(nc.sbuf_tensor("basis", [END_ROW + KPOLY, P], F32R))
        attention(nc, sems, psum, basis, (wq, wk, wv, wo), bq, bk, bv, win, c_basis, c_phase, c_dist, c_ident,
                  c_scale, coef_d, x_t, xt_d, mid_d)
        ffn(nc, sems, psum, basis, c_mask, coef_d, xt_d, mid_d, bo, out_t)


HALF = H // 2
UNITS = {0: [("q", 1)], 1: [("k", 1)], 3: [("o", 0), ("o", 1)], 4: [("q", 2)], 5: [("k", 2)], 6: [("o", 2)],
         7: [("o", 3)], 8: [("q", 3)], 9: [("k", 3)], 11: [("v", 0), ("v", 1)], 12: [("q", 0)],
         13: [("k", 0)], 14: [("v", 2)], 15: [("v", 3)]}
TURNS = {2: [("c", 3)], 7: [("c", 0)], 9: [("x", 0), ("x", 1)], 10: [("x", 2), ("x", 3)], 11: [("c", 1)],
         15: [("c", 2)]}


SPLITS = {13: [(0, 0)], 14: [(0, 1)], 0: [(0, 2)], 1: [(0, 3)], 4: [(1, 0)], 5: [(1, 1)], 6: [(1, 2)], 7: [(1, 3)]}


def slope(h):
    return 2.0 ** (-8.0 / H * (h + 1))


def place(key, s):
    kind, n = key
    if s < HALF:
        return -1 if kind == "o" or key == ("c", 3) else 0
    return 1 if kind in "xv" or (kind in "qk" and n == 0) else 0


def steps_keys(steps, before=True):
    return [key for s in steps for key in UNITS.get(s, []) + TURNS.get(s, []) if before or place(key, s) == 0]


W_PIECES = 8
STACK = 16 * ROLES


PJ_FIRST = [("x", t) for t in range(QT)] + [("q", 0), ("k", 0)] + [("v", t) for t in range(QT)] + \
    steps_keys(range(HALF), before=False)
PJ_BODY = steps_keys([*range(HALF, H), *range(HALF)])
PJ_LAST = [key for key in PJ_BODY if key in (("q", 3), ("k", 3), ("c", 1), ("c", 2))] + \
    [("c", 3)] + [("o", t) for t in range(QT)]
CARRIED = PJ_LAST


def pj_before(key, b):
    if not later(b) and key in PJ_FIRST:
        return 0, PJ_FIRST.index(key)
    n = PJ_BODY.index(key)
    if key in CARRIED and isinstance(b, int) and b == B - 1:
        n = PJ_LAST.index(key)
    return (b if key in CARRIED else b - 1), len(PJ_FIRST) + n


def pj_use(key, b):
    times, rest = pj_before(key, b)
    return rest % 3, times * (len(PJ_BODY) // 3) + rest // 3


def pj_total(key, b):
    times, rest = pj_before(key, b)
    return times * len(PJ_BODY) + rest + 1


def back(b, s, n):
    if s - n >= H:
        return None
    if s - n >= 0:
        return b, s - n
    return (b - 1, s - n + H) if later(b) else None


def active(table, s, carry):
    return [key for key in table.get(s, []) if carry or place(key, s) == 0]


def attention(nc, sems, psum, basis, weights, bq, bk, bv, win, c_basis, c_phase, c_dist, c_ident, c_scale,
              coef_d, x_t, xt_d, mid_d):
    NB = BLOCKS // P
    with ExitStack() as ctx:
        sb = lambda n, s, dt: ctx.enter_context(nc.sbuf_tensor(n, s, dt))
        w_hi = sb("w_hi", [P, 4, KC, D], F32R)
        w_lo = sb("w_lo", [P, 4, KC, D], F32R)
        dist = sb("dist", [P, S], F32)
        ident = sb("ident", [P, P], F32)
        ident16 = sb("ident16", [P, P], F16)
        bv_all = sb("bv_all", [P, D], F32)
        b_qk = sb("b_qk", [P, 2, KC], F32)
        q_scale = sb("q_scale", [P, KC], F32)
        b_scaled = sb("b_scaled", [P, KC], F32)
        x_in = sb("x_in", [P, QT, D], F32)
        xt_hi = sb("xt_hi", [P, KC, S], F32R)
        xt_lo = sb("xt_lo", [P, KC, S], F32R)
        qk_full = sb("qk_full", [P, S], F32)
        parts = sb("parts", [P, 4, S], F32R)
        q_stack = sb("q_stack", [3 * HD, 2, HPC, S], F32R)
        k_stack = sb("k_stack", [3 * HD, 2, HPC, S], F32R)
        v_full = sb("v_full", [P, QT, D], F32)
        v_parts = sb("v_parts", [P, QT, H, 3, HD], BF16)
        ctx_tmp = sb("ctx_tmp", [P, 2, QT, HD], F32)
        stats = sb("stats", [P, QT, 6], F32)
        meanvar = sb("meanvar", [P, QT, 2], F32)
        varp = sb("varp", [P, QT], F32)
        rstd = sb("rstd", [P, QT], F32)
        minus_half = sb("minus_half", [P, QT], F32)
        row_max = sb("row_max", [P, 2, QT], F32)
        neg_max = sb("neg_max", [P, 2, QT], F32)
        row_sum = sb("row_sum", [P, 4, QT], F32)
        inv_sum = sb("inv_sum", [P, 2, QT], F32)
        work = sb("work", [P, 3 * 2 * PROBS], F32)
        probs = work[:, 0:2 * PROBS].rearrange("p (s n) -> p s n", s=2)
        probs16 = work[:, 2 * PROBS:4 * PROBS].bitcast(F16).rearrange("p (s e n) -> p s e n", s=2, e=2)
        probs_t = work[:, 4 * PROBS:6 * PROBS].bitcast(F16).rearrange("p (s n) -> p s n", s=2)
        at = 3 * 2 * D
        w_raw = work[:, 0:at].rearrange("p (s c n) -> p s c n", s=3, c=2)
        points = work[:, at:at + 5 * MATS * NB].rearrange("p (k n) -> p k n", k=5)
        at += 5 * MATS * NB
        phase = work[:, at:at + 2 * MATS * NB].rearrange("p (e n) -> p e n", e=2)
        at += 2 * MATS * NB
        tmp = work[:, at:at + 8 * MATS * NB].rearrange("p (k e n) -> p k e n", k=4, e=2)
        at += 8 * MATS * NB
        poly = work[:, at:at + 8 * MATS * NB].rearrange("p (d e n) -> p d e n", d=4, e=2)
        basis_raw = ctx_tmp[0:END_ROW + KPOLY].rearrange("p a q d -> p (a q d)")[:, 0:P]
        ctx_sb = sb("ctx_sb", [P, 2, QT, P], F32)
        ctx_t = sb("ctx_t", [P, 2, KC, S], F32R)
        poly_hi, poly_lo = [ctx_t[:, e].rearrange("p c n -> p (c n)")[:, 0:8 * MATS * NB]
                            .rearrange("p (d e m n) -> p d e m n", d=4, e=2, m=MATS) for e in range(2)]

        pj_bank, score_bank, av_bank = [psum[0], psum[1], psum[6]], psum[2:4], psum[7]
        pt_bank = [p[:, :].bitcast(F16) for p in psum[4:6]]

        x_ld = sems(ctx, *[f"x_ld{t}" for t in range(QT)])
        w_ld = sems(ctx, "w_ld0", "w_ld1", "w_ld2")
        pj_free = sems(ctx, "pj_free0", "pj_free1", "pj_free2")
        pt_free = sems(ctx, "pt_free0", "pt_free1")
        stacked = [sems(ctx, f"{m}_stacked0", f"{m}_stacked1") for m in "qk"]
        res_ld = sems(ctx, *[f"res_ld{t}" for t in range(QT)])
        res_st = sems(ctx, *[f"res_st{t}" for t in range(QT)])
        (const_ld, points_ld, wh_ready, wl_ready, wl_pool, small_set, poly_step, ph_ready, pl_ready, coef_st,
         pj_full, ln_stats, ln_mv, ln_var, rstd_ready, xn_ready, xh_ready, xt_st,
         full_ready, ql_ready, v_rest, v_mid, vh_ready, v_done, s_full, t_done, nm_ready, p_ready, hi_ready,
         lo_ready, pt_full, av_full, av_read, ctx_ready, ch_ready) = sems(
            ctx, "const_ld", "points_ld", "wh_ready", "wl_ready", "wl_pool", "small_set", "poly_step",
            "ph_ready", "pl_ready", "coef_st", "pj_full", "ln_stats", "ln_mv",
            "ln_var", "rstd_ready", "xn_ready", "xh_ready", "xt_st", "full_ready", "ql_ready", "v_rest", "v_mid",
            "vh_ready", "v_done", "s_full", "t_done", "nm_ready", "p_ready", "p_hi_ready", "p_lo_ready",
            "pt_full", "av_full", "av_read", "ctx_ready", "ch_ready")

        block = ctx.enter_context(nc.Block())

        def w_piece(w, n):
            m, half = divmod(n, 2)
            return w[:, m, 2 * half:2 * half + 2, :]

        @block.tensor
        def _(pe):
            def turn_x(b, t):
                bank, used = pj_use(("x", t), b)
                if later(b) or used:
                    pe.wait_ge(pj_free[bank], used)
                pe.wait_ge(xn_ready, QT * b + t + 1)
                if not later(b) and t == 0:
                    pe.wait_ge(const_ld, 16 * 7)
                for c in range(KC):
                    mm = pe.transpose(pj_bank[bank][:, c * P:(c + 1) * P], x_in[:, t, c * P:(c + 1) * P],
                                      ident[:])
                mm.then_inc(pj_full, 1)

            def product(bank, pairs, some):
                n = len(pairs)
                mm = None
                for k in some:
                    l_hi, l_lo, r_hi, r_lo = pairs[k]
                    pe.matmul(bank[:, :], l_hi, r_hi, start=(k == 0), stop=False)
                    pe.matmul(bank[:, :], l_hi, r_lo, start=False, stop=False)
                    mm = pe.matmul(bank[:, :], l_lo, r_hi, start=False, stop=(k == n - 1))
                if some[-1] == n - 1:
                    mm.then_inc(pj_full, 1)

            def project_qk(b, name, c, some=(0, 1, 2, 3)):
                bank, used = pj_use((name, c), b)
                m = "qk".index(name)
                if some[0] == 0:
                    pe.wait_ge(pj_free[bank], used)
                    if c == 0 and m == 0:
                        x_bank, x_used = pj_use(("x", QT - 1), b)
                        pe.wait_ge(pj_free[x_bank], x_used + 1)
                if not later(b) and c == 0:
                    pe.wait_ge(wl_ready, 2 * m + 2)
                cols = slice(c * P, (c + 1) * P)
                product(pj_bank[bank], [(w_hi[:, m, k, cols], w_lo[:, m, k, cols], xt_hi[:, k, :],
                                         xt_lo[:, k, :]) for k in range(KC)], some)

            def project_v(b, t, some=(0, 1, 2, 3)):
                bank, used = pj_use(("v", t), b)
                if some[0] == 0:
                    pe.wait_ge(pj_free[bank], used)
                    x_bank, x_used = pj_use(("x", t), b)
                    pe.wait_ge(pj_free[x_bank], x_used + 1)
                if not later(b) and t == 0 and some[0] == 0:
                    pe.wait_ge(wl_pool, 2)
                rows = slice(t * P, (t + 1) * P)
                product(pj_bank[bank], [(xt_hi[:, k, rows], xt_lo[:, k, rows], w_hi[:, 2, k, :],
                                         w_lo[:, 2, k, :]) for k in range(KC)], some)

            def scores(b, s, i):
                c, h = divmod(s, HPC)
                if h == 0 and i == 0:
                    pe.wait_ge(stacked[0][c % 2], 2 * STACK * b + STACK * (c // 2 + 1))
                    pe.wait_ge(stacked[1][c % 2], 2 * STACK * b + STACK * (c // 2 + 1))
                if later(b) or 4 * s + i >= 2:
                    pe.wait_ge(t_done, 64 * b + 4 * s + i - 1)
                n = max(2, i + 1) * P
                pe.matmul(score_bank[i % 2][:, 0:n], q_stack[:, c % 2, h, i * P:(i + 1) * P],
                          k_stack[:, c % 2, h, 0:n], start=True, stop=True).then_inc(s_full, 1)

            def turn_probs(b, s, i):
                if i == 0:
                    if not later(b) and s == 0:
                        pe.wait_ge(small_set, 2)
                    pe.wait_ge(hi_ready, H * b + s + 1)
                    pe.wait_ge(lo_ready, H * b + s + 1)
                if later(b) or 2 * s + i // 2 > 0:
                    pe.wait_ge(pt_free[i % 2], 2 * (H * b + s) + i // 2)
                n = i + 1
                for part in range(2):
                    for k in range(n):
                        mm = pe.transpose(pt_bank[i % 2][:, (part * n + k) * P:(part * n + k + 1) * P],
                                          probs16[:, s % 2, part, OFF[i] + k * P:OFF[i] + (k + 1) * P],
                                          ident16[:])
                mm.then_inc(pt_full, 1)

            def weigh_values(b, s, i):
                if i == 0:
                    if later(b) or s >= 1:
                        pe.wait_ge(av_read, H * b + s)
                    if s % HALF == 0:
                        pe.wait_ge(v_done, 2 * QT * b + QT * (s // HALF + 1))
                bank = av_bank
                pe.wait_ge(pt_free[i % 2], 2 * (H * b + s) + i // 2 + 1)
                n = i + 1
                for k in range(n):
                    at = 2 * OFF[i] + k * P
                    pe.matmul(bank[:, i * 96:(i + 1) * 96], probs_t[:, s % 2, at:at + P],
                              v_parts[:, k, s, :, :], start=(k == 0), stop=False)
                    at += n * P
                    mm = pe.matmul(bank[:, i * 96:i * 96 + 64], probs_t[:, s % 2, at:at + P],
                                   v_parts[:, k, s, 0:2, :], start=False, stop=(k == n - 1))
                if i == QT - 1:
                    mm.then_inc(av_full, 1)

            def turn_ctx(b, c):
                bank, used = pj_use(("c", c), b)
                pe.wait_ge(pj_free[bank], used)
                pe.wait_ge(ctx_ready, H * b + HPC * (c + 1))
                for q in range(QT):
                    mm = pe.transpose(pj_bank[bank][:, q * P:(q + 1) * P], ctx_sb[:, c % 2, q, :], ident[:])
                mm.then_inc(pj_full, 1)

            def project_out(b, q, some=(0, 1, 2, 3)):
                bank, used = pj_use(("o", q), b)
                if some[0] == 0:
                    pe.wait_ge(pj_free[bank], used)
                    if q == 0:
                        c_bank, c_used = pj_use(("c", KC - 1), b)
                        pe.wait_ge(pj_free[c_bank], c_used + 1)
                        if not later(b):
                            pe.wait_ge(wl_pool, 4)
                rows = slice(q * P, (q + 1) * P)
                product(pj_bank[bank], [(ctx_t[:, 0, c, rows], ctx_t[:, 1, c, rows],
                                         w_hi[:, 3, c, :], w_lo[:, 3, c, :]) for c in range(KC)], some)

            def unit(b, s, key, some=(0, 1, 2, 3)):
                of, (kind, n) = b + place(key, s), key
                if kind in "qk":
                    project_qk(of, kind, n, some)
                elif kind == "v":
                    project_v(of, n, some)
                else:
                    project_out(of, n, some)

            def step(b, s, carry):
                own, turned, weighed = back(b, s, 0), back(b, s, 2), back(b, s, 3)
                units, turns = active(UNITS, s, carry), active(TURNS, s, carry)
                early, rest = ([], units) if s == 3 else (units[:1], units[1:])
                for i in range(2):
                    if own:
                        scores(b, s, i)
                for i in range(2):
                    if weighed:
                        weigh_values(*weighed, i)
                for key in early:
                    unit(b, s, key, (0, 1))
                for i in range(2, QT):
                    if own:
                        scores(b, s, i)
                if turned:
                    turn_probs(*turned, 0)
                for key in early:
                    unit(b, s, key, (2,))
                if turned:
                    turn_probs(*turned, 1)
                for i in range(2, QT):
                    if weighed:
                        weigh_values(*weighed, i)
                for key in early:
                    unit(b, s, key, (3,))
                for i in range(2, QT):
                    if turned:
                        turn_probs(*turned, i)
                for key in rest:
                    unit(b, s, key)
                for key in turns:
                    (turn_x if key[0] == "x" else turn_ctx)(b + place(key, s), key[1])

            for t in range(QT):
                turn_x(0, t)
            project_qk(0, "q", 0)
            project_qk(0, "k", 0)
            for t in range(QT):
                project_v(0, t)
            for s in range(HALF):
                step(0, s, False)
            with pe.Fori(1, B) as b:
                for s in range(HALF, H):
                    step(b - 1, s, True)
                for s in range(HALF):
                    step(b, s, True)
            for s in range(HALF, H + 3):
                step(B - 1, s, False)
            turn_ctx(B - 1, KC - 1)
            for q in range(QT):
                project_out(B - 1, q)

        @block.vector
        def _(dve):
            def norm_stats(b, tiles):
                for t in tiles:
                    dve.wait_ge(x_ld[t], 16 * b + 16)
                    dve.bn_stats(stats[:, t, :], x_in[:, t, :]).then_inc(ln_stats, 1)
                dve.wait_ge(ln_stats, QT * b + tiles[-1] + 1)
                dve.nop(nofuse=True)
                for t in tiles:
                    dve.bn_aggr(meanvar[:, t, :], stats[:, t, :]).then_inc(ln_mv, 1)
                dve.wait_ge(ln_mv, QT * b + tiles[-1] + 1)
                two = slice(tiles[0], tiles[-1] + 1)
                dve.tensor_scalar(varp[:, two], meanvar[:, two, 1], EPS, None, ALU.add).then_inc(ln_var, 1)

            def norm_apply(b, t):
                if t % 2 == 0:
                    dve.wait_ge(rstd_ready, 2 * b + t // 2 + 1)
                dve.tensor_scalar(x_in[:, t, :], x_in[:, t, :], meanvar[:, t, 0:1], rstd[:, t:t + 1],
                                  ALU.subtract, ALU.mult).then_inc(xn_ready, 1)

            def x_low(b, t):
                bank, _ = pj_use(("x", t), b)
                rows = slice(t * P, (t + 1) * P)
                dve.wait_ge(xh_ready, QT * b + t + 1)
                if later(b) and t == 0:
                    dve.wait_ge(xt_st, 32 * b)
                dve.tensor_tensor(xt_lo[:, :, rows], pj_bank[bank][:, :].rearrange("p (c n) -> p c n", c=KC),
                                  xt_hi[:, :, rows].bitcast(F32), ALU.subtract).then_inc(pj_free[bank], 1)

            def v_take(b, t):
                bank, _ = pj_use(("v", t), b)
                dve.wait_ge(pj_full, pj_total(("v", t), b))
                if later(b) and t == 0:
                    dve.wait_ge(v_done, 2 * QT * b)
                dve.tensor_tensor(v_full[:, t, :], pj_bank[bank][:, :], bv_all[:], ALU.add
                                  ).then_inc(pj_free[bank], 1)

            def v_split(b, half, t):
                heads = slice(half * HALF, (half + 1) * HALF)
                full = v_full[:, t, :].rearrange("p (h d) -> p h d", h=H)[:, heads]
                n = 2 * QT * b + QT * half + t + 1
                dve.wait_ge(vh_ready, n)
                dve.tensor_tensor(full, full, v_parts[:, t, heads, 0, :], ALU.subtract).then_inc(v_rest, 1)
                dve.wait_ge(v_rest, n)
                dve.tensor_copy(v_parts[:, t, heads, 1, :], full).then_inc(v_mid, 1)
                dve.wait_ge(v_mid, n)
                dve.tensor_tensor(v_parts[:, t, heads, 2, :], full, v_parts[:, t, heads, 1, :],
                                  ALU.subtract).then_inc(v_done, 1)

            def bias_and_max(b, s, tiles):
                if (later(b) or s >= 2) and tiles[0] == 0:
                    dve.wait_ge(lo_ready, H * b + s - 1)
                for i in tiles:
                    n = (i + 1) * P
                    dve.wait_ge(s_full, 64 * b + 4 * s + i + 1)
                    dve.nop(nofuse=True)
                    dve.tensor_tensor_reduce(
                        probs[:, s % 2, OFF[i]:OFF[i] + n], score_bank[i % 2][:, 0:n], dist[:, S - n:S],
                        1.0, -3.4e38, ALU.add, ALU.max, row_max[:, s % 2, i:i + 1]).then_inc(t_done, 1)

            def negate_max(b, s):
                dve.wait_ge(t_done, 64 * b + 4 * s + 4)
                dve.tensor_scalar(neg_max[:, s % 2, :], row_max[:, s % 2, :], -slope(s), None,
                                  ALU.mult).then_inc(nm_ready, 1)

            def probs_high(b, s):
                dve.wait_ge(p_ready, H * b + s + 1)
                if later(b) or s >= 2:
                    dve.wait_ge(pt_full, 4 * (H * b + s - 1))
                dve.tensor_copy(probs16[:, s % 2, 0, :], probs[:, s % 2, :]).then_inc(hi_ready, 1)

            def take_turned(b, s, i):
                n = 2 * (i + 1) * P
                dve.wait_ge(pt_full, 4 * (H * b + s) + i + 1)
                if later(b) or s >= 2:
                    dve.wait_ge(av_full, H * b + s - 1)
                dve.tensor_copy(probs_t[:, s % 2, 2 * OFF[i]:2 * OFF[i] + n],
                                pt_bank[i % 2][:, 0:n]).then_inc(pt_free[i % 2], 1)

            def normalize(b, s):
                c, h = divmod(s, HPC)
                dve.wait_ge(av_full, H * b + s + 1)
                if later(b) or s >= 2:
                    dve.wait_ge(ctx_ready, H * b + s - 1)
                dve.reciprocal(inv_sum[:, s % 2, :], row_sum[:, s % 4, :])
                dve.tensor_reduce(ctx_tmp[:, s % 2],
                                  av_bank[:, 0:QT * 96].rearrange("p (q t d) -> p q d t", q=QT, t=3),
                                  AX_X, ALU.add).then_inc(av_read, 1)
                dve.wait_ge(av_read, H * b + s + 1)
                if h == 0 and (later(b) or c >= 2):
                    dve.wait_ge(pj_full, pj_total(("c", (c - 2) % KC), b if c >= 2 else b - 1))
                dve.tensor_tensor(ctx_sb[:, c % 2, :, h * HD:(h + 1) * HD], ctx_tmp[:, s % 2],
                                  inv_sum[:, s % 2, :].unsqueeze(2).broadcast_to([P, QT, HD]),
                                  ALU.mult).then_inc(ctx_ready, 1)

            def ctx_low(b, c):
                bank, _ = pj_use(("c", c), b)
                dve.wait_ge(ch_ready, KC * b + c + 1)
                dve.tensor_tensor(ctx_t[:, 1, c, :], pj_bank[bank][:, :], ctx_t[:, 0, c, :].bitcast(F32),
                                  ALU.subtract).then_inc(pj_free[bank], 1)

            def add_residual(b, q):
                bank, _ = pj_use(("o", q), b)
                dve.wait_ge(pj_full, pj_total(("o", q), b))
                dve.wait_ge(res_ld[q], 16 * b + 16)
                dve.tensor_tensor(x_in[:, q, :], pj_bank[bank][:, :], x_in[:, q, :], ALU.add
                                  ).then_inc(pj_free[bank], 1)

            def step(b, s, carry, carried):
                halved, turned, weighed = back(b, s, 1), back(b, s, 2), back(b, s, 3)
                last = (s - 1) % H
                before = b - 1 if s == 0 else b
                if s > H or (s == 0 and not later(b)):
                    units = turns = []
                else:
                    units = [(before + place(key, last), key) for key in active(UNITS, last, carried)]
                    turns = [(before + place(key, last), key) for key in active(TURNS, last, carried)]
                if s < H:
                    bias_and_max(b, s, (0, 1))
                for of, (kind, n) in units:
                    if kind == "v":
                        v_take(of, n)
                    elif kind == "o":
                        add_residual(of, n)
                if halved:
                    probs_high(*halved)
                if s < H:
                    bias_and_max(b, s, (2, 3))
                    negate_max(b, s)
                if s == 3:
                    for of, (_, c) in turns:
                        ctx_low(of, c)
                if turned:
                    take_turned(*turned, 0)
                    take_turned(*turned, 1)
                if weighed:
                    normalize(*weighed)
                if carry and s == 9:
                    norm_apply(b + 1, 0)
                    norm_apply(b + 1, 1)
                if carry and s == 10:
                    norm_apply(b + 1, 2)
                    norm_apply(b + 1, 3)
                for of, (kind, n) in turns if s != 3 else []:
                    (x_low if kind == "x" else ctx_low)(of, n)
                if carry and s == HALF - 1:
                    add_residual(b - 1, QT - 1)
                if carry and s in (8, 9):
                    norm_stats(b + 1, (2 * s - 16, 2 * s - 15))
                for half, t in SPLITS.get(s, []):
                    if s >= HALF:
                        if carry:
                            v_split(b + 1, half, t)
                    elif carry or half:
                        v_split(b, half, t)

            def w_low(n):
                dve.wait_ge(wh_ready, n + 1)
                dve.tensor_tensor(w_piece(w_lo, n), w_raw[:, n % 3], w_piece(w_hi, n).bitcast(F32),
                                  ALU.subtract).then_inc(wl_ready, 1)

            def polynomials():
                steps = [0]

                def then(ins):
                    steps[0] += 1
                    ins.then_inc(poly_step, 1)
                    dve.wait_ge(poly_step, steps[0])

                p0, p1, p2, p3 = [points[:, k:k + 2, :] for k in range(4)]
                c1, c2, u, v = [tmp[:, k] for k in range(4)]
                a0, a1, a2, a3 = [poly[:, d] for d in range(4)]
                dve.wait_ge(points_ld, 32)
                dve.tensor_tensor(c1, p2, p0, ALU.subtract)
                dve.tensor_tensor(u, p3, p0, ALU.subtract)
                then(dve.tensor_tensor(v, p1, p2, ALU.subtract))
                dve.scalar_tensor_tensor(a3, v, 3.0, u, ALU.mult, ALU.add)
                then(dve.scalar_tensor_tensor(c2, p0, 2.0, p3, ALU.mult, ALU.subtract))
                then(dve.scalar_tensor_tensor(c2, p1, -5.0, c2, ALU.mult, ALU.add))
                dve.tensor_tensor(v, a3, phase, ALU.mult)
                then(dve.scalar_tensor_tensor(c2, p2, 4.0, c2, ALU.mult, ALU.add))
                then(dve.tensor_tensor(a2, v, c2, ALU.add))
                then(dve.tensor_tensor(a1, a2, phase, ALU.mult))
                then(dve.tensor_tensor(a1, a1, c1, ALU.add))
                then(dve.tensor_tensor(a0, a1, phase, ALU.mult))
                dve.scalar_tensor_tensor(a0, p1, 2.0, a0, ALU.mult, ALU.add)
                then(dve.tensor_tensor(a2, a2, v, ALU.add))
                then(dve.tensor_tensor(u, a2, phase, ALU.mult))
                dve.tensor_tensor(a2, a2, v, ALU.add)
                then(dve.tensor_tensor(a1, a1, u, ALU.add))

            dve.memset(minus_half[:], -0.5).then_inc(small_set, 1)
            norm_stats(0, (0, 1))
            w_low(0)
            norm_apply(0, 0)
            norm_apply(0, 1)
            w_low(1)
            x_low(0, 0)
            x_low(0, 1)
            norm_stats(0, (2, 3))
            dve.wait_ge(const_ld, 16 * 7)
            dve.tensor_copy(ident16[:], ident[:]).then_inc(small_set, 1)
            dve.tensor_tensor(b_scaled[:], b_qk[:, 0, :], q_scale[:], ALU.mult).then_inc(small_set, 1)
            norm_apply(0, 2)
            norm_apply(0, 3)
            x_low(0, 2)
            x_low(0, 3)
            w_low(2)
            w_low(3)
            polynomials()
            for t in range(QT):
                v_take(0, t)
            for t in range(QT):
                v_split(0, 0, t)
            dve.wait_ge(ph_ready, 1)
            dve.tensor_tensor(poly_lo.rearrange("p d e m n -> p (d e m n)"),
                              poly.rearrange("p d e n -> p (d e n)"),
                              poly_hi.rearrange("p d e m n -> p (d e m n)").bitcast(F32),
                              ALU.subtract).then_inc(pl_ready, 1)
            dve.wait_ge(wl_pool, 4)
            dve.wait_ge(wl_ready, 4)
            dve.wait_ge(pl_ready, 1)
            for s in range(HALF):
                step(0, s, False, False)
            with dve.Fori(1, B) as b:
                for s in range(HALF, H):
                    step(b - 1, s, True, s > HALF)
                for s in range(HALF):
                    step(b, s, True, True)
            for s in range(HALF, H + 3):
                step(B - 1, s, False, False)
            ctx_low(B - 1, KC - 1)
            for q in range(QT):
                add_residual(B - 1, q)

        @block.scalar
        def _(act):
            def x_high(b, t):
                bank, _ = pj_use(("x", t), b)
                act.wait_ge(pj_full, pj_total(("x", t), b))
                if later(b) and t == 0:
                    act.wait_ge(xt_st, 32 * b)
                act.copy(xt_hi[:, :, t * P:(t + 1) * P],
                         pj_bank[bank][:, :].rearrange("p (c n) -> p c n", c=KC)).then_inc(xh_ready, 1)

            def qk_high(b, name, c):
                m = "qk".index(name)
                bank, _ = pj_use((name, c), b)
                scale = q_scale[:, c:c + 1] if m == 0 else 1.0
                bias = b_scaled[:, c:c + 1] if m == 0 else b_qk[:, 1, c:c + 1]
                act.wait_ge(pj_full, pj_total((name, c), b))
                if later(b) or c > 0 or m > 0:
                    act.wait_ge(ql_ready, 8 * b + 2 * c + m)
                act.activation(qk_full[:], pj_bank[bank][:, :], ACT.Identity, bias=bias,
                               scale=scale).then_inc(full_ready, 1)
                if c > 0:
                    act.wait_ge(stacked[m][(c - 1) % 2], 2 * STACK * b + STACK * ((c - 1) // 2 + 1))
                elif later(b):
                    act.wait_ge(stacked[m][1], 2 * STACK * b)
                act.activation(parts[:, 2 * m, :], pj_bank[bank][:, :], ACT.Identity, bias=bias,
                               scale=scale).then_inc(pj_free[bank], 1)

            def v_high(b, half, t):
                heads = slice(half * HALF, (half + 1) * HALF)
                if half == 0:
                    bank, used = pj_use(("v", t), b)
                    act.wait_ge(pj_free[bank], used + 1)
                if (later(b) or half) and t == 0:
                    if later(b):
                        act.wait_ge(av_full, H * (b - 1) + HALF * (half + 1))
                act.copy(v_parts[:, t, heads, 0, :],
                         v_full[:, t, :].rearrange("p (h d) -> p h d", h=H)[:, heads]).then_inc(vh_ready, 1)

            def exponentials(b, s):
                act.wait_ge(nm_ready, H * b + s + 1)
                if later(b) or s >= 4:
                    act.wait_ge(av_read, H * b + s - 3)
                for i in range(QT):
                    tile = probs[:, s % 2, OFF[i]:OFF[i] + (i + 1) * P]
                    e = act.activation(tile, tile, ACT.Exp, bias=neg_max[:, s % 2, i:i + 1],
                                       scale=slope(s), accum_out=row_sum[:, s % 4, i:i + 1])
                e.then_inc(p_ready, 1)

            def take_turned(b, s, i):
                n = 2 * (i + 1) * P
                act.wait_ge(pt_full, 4 * (H * b + s) + i + 1)
                if later(b) or s >= 2:
                    act.wait_ge(av_full, H * b + s - 1)
                act.copy(probs_t[:, s % 2, 2 * OFF[i]:2 * OFF[i] + n],
                         pt_bank[i % 2][:, 0:n]).then_inc(pt_free[i % 2], 1)

            def ctx_high(b, c):
                bank, _ = pj_use(("c", c), b)
                act.wait_ge(pj_full, pj_total(("c", c), b))
                if not later(b) and c == 0:
                    act.wait_ge(coef_st, 16 * 2 * ROLES * MATS)
                act.copy(ctx_t[:, 0, c, :], pj_bank[bank][:, :]).then_inc(ch_ready, 1)

            def step(b, s, carry):
                turned = back(b, s, 2)
                if s < H:
                    exponentials(b, s)
                if turned:
                    take_turned(*turned, 2)
                    take_turned(*turned, 3)
                for key in active(UNITS, s, carry):
                    if key[0] in "qk":
                        qk_high(b + place(key, s), *key)
                for key in active(TURNS, s, carry):
                    (x_high if key[0] == "x" else ctx_high)(b + place(key, s), key[1])
                for half, t in SPLITS.get((s + 1) % H, []) if s < H else []:
                    if s >= HALF - 1 and carry and half == 0:
                        v_high(b + 1, half, t)
                    elif s < HALF - 1 and (carry or half):
                        v_high(b, half, t)

            def w_high(n):
                act.wait_ge(w_ld[n % 3], 16 * (n // 3 + 1))
                act.copy(w_piece(w_hi, n), w_raw[:, n % 3]).then_inc(wh_ready, 1)

            act.dma_start(ident[:], c_ident).then_inc(const_ld, 16)
            act.dma_start(b_qk[:, 0, :], bq).then_inc(const_ld, 16)
            act.dma_start(b_qk[:, 1, :], bk).then_inc(const_ld, 16)
            act.dma_start(bv_all[:], bv.partition_broadcast(P)).then_inc(const_ld, 16)
            act.dma_start(basis_raw, c_basis).then_inc(const_ld, 16)
            act.dma_start(dist[:], c_dist).then_inc(const_ld, 16)
            act.dma_start(q_scale[:], c_scale).then_inc(const_ld, 16)
            act.dma_start(points, win).then_inc(points_ld, 16)
            act.dma_start(phase, c_phase).then_inc(points_ld, 16)
            w_high(0)
            w_high(1)
            x_high(0, 0)
            x_high(0, 1)
            w_high(2)
            x_high(0, 2)
            x_high(0, 3)
            w_high(3)
            act.wait_ge(small_set, 3)
            qk_high(0, "q", 0)
            w_high(4)
            w_high(5)
            qk_high(0, "k", 0)
            act.copy(basis[:], basis_raw)
            for n in range(6, W_PIECES):
                w_high(n)
            act.wait_ge(poly_step, 11)
            act.copy(poly_hi.rearrange("p d e m n -> p (d e m n)"),
                     poly.rearrange("p d e n -> p (d e n)")).then_inc(ph_ready, 1)
            for t in range(QT):
                v_high(0, 0, t)
            for s in range(HALF):
                step(0, s, False)
            with act.Fori(1, B) as b:
                for s in range(HALF, H):
                    step(b - 1, s, True)
                for s in range(HALF):
                    step(b, s, True)
            for s in range(HALF, H + 3):
                step(B - 1, s, False)
            ctx_high(B - 1, KC - 1)

        @block.gpsimd
        def _(pool):
            def inverse_std(b, n):
                two = slice(2 * n, 2 * n + 2)
                pool.wait_ge(ln_var, 2 * b + n + 1)
                pool.tensor_tensor(rstd[:, two], varp[:, two], minus_half[:, two], ALU.pow
                                   ).then_inc(rstd_ready, 1)

            def qk_low(b, name, c):
                m = "qk".index(name)
                bank, used = pj_use((name, c), b)
                pool.wait_ge(pj_free[bank], used + 1)
                pool.tensor_tensor(parts[:, 2 * m + 1, :], qk_full[:], parts[:, 2 * m, :].bitcast(F32),
                                   ALU.subtract).then_inc(ql_ready, 1)

            def probs_low(b, s):
                pool.wait_ge(hi_ready, H * b + s + 1)
                pool.tensor_tensor(probs16[:, s % 2, 1, :], probs[:, s % 2, :], probs16[:, s % 2, 0, :],
                                   ALU.subtract).then_inc(lo_ready, 1)

            def step(b, s, carry, carried):
                halved = back(b, s, 1)
                if carry and s in (9, 10):
                    inverse_std(b + 1, s - 9)
                if halved:
                    probs_low(*halved)
                if s < H and (s or later(b)):
                    for key in active(UNITS, (s - 1) % H, carried):
                        if key[0] in "qk":
                            qk_low(b + place(key, s - 1), *key)

            pool.wait_ge(small_set, 1)
            inverse_std(0, 0)
            inverse_std(0, 1)
            for n in range(4, 6):
                pool.wait_ge(wh_ready, n + 1)
                pool.tensor_tensor(w_piece(w_lo, n), w_raw[:, n % 3], w_piece(w_hi, n).bitcast(F32),
                                   ALU.subtract).then_inc(wl_pool, 1)
            qk_low(0, "q", 0)
            qk_low(0, "k", 0)
            for n in range(6, W_PIECES):
                pool.wait_ge(wh_ready, n + 1)
                pool.tensor_tensor(w_piece(w_lo, n), w_raw[:, n % 3], w_piece(w_hi, n).bitcast(F32),
                                   ALU.subtract).then_inc(wl_pool, 1)
            for s in range(HALF):
                step(0, s, False, False)
            with pool.Fori(1, B) as b:
                for s in range(HALF, H):
                    step(b - 1, s, True, s > HALF)
                for s in range(HALF):
                    step(b, s, True, True)
            for s in range(HALF, H + 1):
                step(B - 1, s, False, False)

        @block.sync
        def _(sp):
            def load_x(b, t):
                sp.dma_start(x_in[:, t, :], rows_of(x_t, QT * b + t)).then_inc(x_ld[t], 16)

            def store_xt(b):
                bank, used = pj_use(("x", QT - 1), b)
                sp.wait_ge(pj_free[bank], used + 1)
                sp.nop(nofuse=True)
                for e, part in enumerate((xt_hi, xt_lo)):
                    sp.dma_start(rows_of(xt_d, 2 * b + e), part[:].rearrange("p c n -> p (c n)").bitcast(F32)
                                 ).then_inc(xt_st, 16)

            def stack(b, c):
                if later(b) or c >= 2:
                    sp.wait_ge(s_full, 64 * b + 16 * (c - 1))
                    sp.nop(nofuse=True)
                for m, stacks in ((0, q_stack), (1, k_stack)):
                    sp.wait_ge(ql_ready, 8 * b + 2 * c + m + 1)
                    sp.nop(nofuse=True)
                    for role, low in enumerate(((0, 1, 0), (0, 0, 1))[m]):
                        sp.dma_start(
                            stacks[role * HD:(role + 1) * HD, c % 2].rearrange("d h n -> d (h n)").bitcast(F32),
                            parts[:, 2 * m + low, :].bitcast(F32)).then_inc(stacked[m][c % 2], 16)

            def load_residual(b, q):
                sp.dma_start(x_in[:, q, :], rows_of(x_t, QT * b + q)).then_inc(res_ld[q], 16)

            def store_sum(b, q):
                bank, used = pj_use(("o", q), b)
                sp.wait_ge(pj_free[bank], used + 1)
                sp.nop(nofuse=True)
                sp.dma_start(rows_of(mid_d, QT * b + q), x_in[:, q, :]).then_inc(res_st[q], 16)

            def load_piece(n):
                m, half = divmod(n, 2)
                if n >= 7:
                    sp.wait_ge(wl_pool, n - 6)
                elif n >= 3:
                    sp.wait_ge(wl_ready, n - 2)
                src = weights[m].rearrange("(c p) n -> p c n", p=P)
                sp.dma_start(w_raw[:, n % 3], src[:, 2 * half:2 * half + 2, :]).then_inc(w_ld[n % 3], 16)

            load_x(0, 0)
            load_x(0, 1)
            for n in range(3):
                load_piece(n)
            load_x(0, 2)
            load_x(0, 3)
            for n in range(3, W_PIECES):
                load_piece(n)
            store_xt(0)
            stack(0, 0)
            sp.wait_ge(pl_ready, 1)
            for e in range(2):
                for role, part in enumerate((poly_hi, poly_hi, poly_lo)):
                    for m in range(MATS):
                        sp.dma_start(
                            coef_d[e, 4 * role:4 * role + 4, m, :].rearrange("d (p n) -> p d n", p=P),
                            part[:, :, e, m, :].bitcast(F32)).then_inc(coef_st, 16)
            stack(0, 1)
            sp.wait_ge(coef_st, 16 * 2 * ROLES * MATS)
            stack(0, 2)
            with sp.Fori(1, B) as b:
                for t in range(QT):
                    load_x(b, t)
                stack(b - 1, 3)
                for q in range(QT):
                    sp.wait_ge(pj_full, pj_total(("x", q), b))
                    sp.nop(nofuse=True)
                    load_residual(b - 1, q)
                store_xt(b)
                stack(b, 0)
                stack(b, 1)
                store_sum(b - 1, 0)
                store_sum(b - 1, 1)
                stack(b, 2)
                store_sum(b - 1, 2)
                store_sum(b - 1, 3)
                for q in range(QT):
                    sp.wait_ge(res_st[q], 16 * b)
                sp.nop(nofuse=True)
            for q in range(QT):
                load_residual(B - 1, q)
            stack(B - 1, 3)
            for q in range(QT):
                store_sum(B - 1, q)
            for q in range(QT):
                sp.wait_ge(res_st[q], 16 * B)
            sp.wait_ge(xt_st, 32 * B)


def ffn(nc, sems, psum, basis, c_mask, coef_d, xt_d, mid_d, bo, out_t):
    NT = B * QT
    with ExitStack() as ctx:
        sb = lambda n, s, dt: ctx.enter_context(nc.sbuf_tensor(n, s, dt))
        xt = sb("xt", [P, B, 2, KC, S], F32R)
        acc = sb("acc", [P, NT, D], F32)
        w_hi = sb("fw_hi", [P, 2, MATS, PW], F32R)
        w_lo = sb("fw_lo", [P, 2, MATS, PW], F32R)
        in_hi = sb("in_hi", [P, 2, 2, S], F32R)
        in_lo = sb("in_lo", [P, 2, 2, S], F32R)
        silu = sb("silu", [P, 2, S], F32)
        inner = sb("inner", [P, 2, S], F32)
        w_new = sb("w_new", [P, 2, 512], F32)
        coef = sb("coef", [END_ROW + KPOLY, 2, MATS, PW], F32R)
        mask = sb("mask", [P, 2, 2, PW], U8)
        bo_all = sb("bo_all", [P, D], F32)

        gate_bank, up_bank, down_bank = psum[0:2], psum[2:4], psum[4:6]
        start_bank, end_bank = psum[6], psum[7]
        def last(pair):
            return isinstance(pair, int) and pair == PAIRS - 1

        GROUPS = MATS * 2

        xt_ld = sems(ctx, *[f"xt_ld{b}" for b in range(B)])
        acc_ld = sems(ctx, *[f"acc_ld{b}" for b in range(B)])
        coef_ld = [sems(ctx, *[f"coef_ld{sl}_{m}" for m in range(MATS)]) for sl in range(2)]
        mask_ld = sems(ctx, "mask_ld0", "mask_ld1")
        (bo_ld, bo_added, ends_full, start_read, w_merged, wh_ready, wl_ready, gate_full, up_full, silu_ready,
         inner_ready, ih_ready, il_ready, down_full, down_added, stored) = sems(
            ctx, "bo_ld", "bo_added", "ends_full", "start_read", "w_merged", "wh_ready", "wl_ready", "gate_full",
            "up_full", "silu_ready", "inner_ready", "ih_ready", "il_ready", "down_full", "down_added", "stored")

        block = ctx.enter_context(nc.Block())

        WGEN = {0: (0, 1), 1: (2, 3), 2: (4, 5), 3: ()}

        @block.tensor
        def _(pe):
            def make(pair, g, sl):
                m, half = divmod(g, 2)
                cols = slice(half * 512, (half + 1) * 512)
                if half == 0:
                    pe.wait_ge(coef_ld[sl][m], 16 * pair + 32 - 16 * sl)
                if later(pair) or g:
                    pe.wait_ge(w_merged, GROUPS * pair + g)
                pe.matmul(start_bank[:, :], basis[0:KPOLY, :], coef[0:KPOLY, sl, m, cols], start=True, stop=True)
                pe.matmul(end_bank[:, :], basis[END_ROW:END_ROW + KPOLY, :],
                          coef[END_ROW:END_ROW + KPOLY, sl, m, cols], start=True, stop=True).then_inc(ends_full, 1)

            def gate_or_up(m, pair, sl, t, j):
                k = 4 * pair + t
                if j == 0 and m == 0 and not later(pair):
                    pe.wait_ge(xt_ld[t], 16)
                if t == 0 and j == 0:
                    pe.wait_ge(wl_ready, GROUPS * pair + 2 * (m + 1))
                bank, full = ((gate_bank, gate_full), (up_bank, up_full))[m]
                if later(k):
                    pe.wait_ge((silu_ready, inner_ready)[m], 2 * k + j - 1)
                for q in range(KC):
                    cols = slice(q * 2 * P + j * P, q * 2 * P + (j + 1) * P)
                    hi, lo = w_hi[:, sl, m, cols], w_lo[:, sl, m, cols]
                    pe.matmul(bank[j][:, :], hi, xt[:, t, 0, q, :], start=(q == 0), stop=False)
                    pe.matmul(bank[j][:, :], hi, xt[:, t, 1, q, :], start=False, stop=False)
                    mm = pe.matmul(bank[j][:, :], lo, xt[:, t, 0, q, :], start=False, stop=(q == KC - 1))
                mm.then_inc(full, 1)

            def down(pair, sl, t):
                k = 4 * pair + t
                pe.wait_ge(il_ready, 2 * k + 2)
                if t == 0:
                    pe.wait_ge(wl_ready, GROUPS * pair + GROUPS)
                for i in range(QT):
                    bank = down_bank[i % 2]
                    if later(k) or i >= 2:
                        pe.wait_ge(down_added, QT * k + i - 1)
                    for j in range(2):
                        hi, lo = in_hi[:, t % 2, j, i * P:(i + 1) * P], in_lo[:, t % 2, j, i * P:(i + 1) * P]
                        r_hi, r_lo = [w[:, sl, 2, j * 512:(j + 1) * 512] for w in (w_hi, w_lo)]
                        pe.matmul(bank[:, :], hi, r_hi, start=(j == 0), stop=False)
                        pe.matmul(bank[:, :], hi, r_lo, start=False, stop=False)
                        mm = pe.matmul(bank[:, :], lo, r_hi, start=False, stop=(j == 1))
                    mm.then_inc(down_full, 1)

            def body(it):
                for sl in range(2):
                    pair = 2 * it + sl
                    for t in range(B):
                        k = 4 * pair + t
                        made = WGEN[t] if not last(pair) else ()
                        for j in range(2):
                            gate_or_up(0, pair, sl, t, j)
                            if not later(k):
                                make(0, 2 + j, 0)
                        for j in range(2):
                            gate_or_up(1, pair, sl, t, j)
                            if not later(k):
                                make(0, 4 + j, 0)
                        for g in made[:1]:
                            make(pair + 1, g, 1 - sl)
                        if t:
                            down(pair, sl, t - 1)
                        elif later(k):
                            down(pair - 1, 1 - sl, B - 1)
                        for g in made[1:]:
                            make(pair + 1, g, 1 - sl)

            make(0, 0, 0)
            make(0, 1, 0)
            body(0)
            with pe.Fori(1, PAIRS // 2 - 1) as it:
                body(it)
            body(PAIRS // 2 - 1)
            down(PAIRS - 1, 1, B - 1)

        @block.scalar
        def _(act):
            def start_part(pair, g):
                act.wait_ge(ends_full, GROUPS * pair + g + 1)
                if later(pair) or g >= 2:
                    act.wait_ge(wl_ready, GROUPS * pair + g - 1)
                act.copy(w_new[:, g % 2, :], start_bank[:, :]).then_inc(start_read, 1)

            def high(pair, g, sl):
                m, half = divmod(g, 2)
                act.wait_ge(w_merged, GROUPS * pair + g + 1)
                act.copy(w_hi[:, sl, m, half * 512:(half + 1) * 512], w_new[:, g % 2, :]).then_inc(wh_ready, 1)

            def gated(k, t, j):
                act.wait_ge(gate_full, 2 * k + j + 1)
                if later(k):
                    act.wait_ge(inner_ready, 2 * k + j - 1)
                act.activation(silu[:, j, :], gate_bank[j][:, :], ACT.Silu).then_inc(silu_ready, 1)

            def inner_high(k, t, j):
                act.wait_ge(inner_ready, 2 * k + j + 1)
                if not isinstance(k, int) or k >= 2:
                    act.wait_ge(down_full, QT * (k - 1))
                act.copy(in_hi[:, t % 2, j, :], inner[:, j, :]).then_inc(ih_ready, 1)

            def body(it):
                for sl in range(2):
                    pair = 2 * it + sl
                    for t in range(B):
                        k = 4 * pair + t
                        made = WGEN[t] if not last(pair) else ()
                        for j in range(2):
                            gated(k, t, j)
                            if not later(k):
                                start_part(0, 2 + j)
                                high(0, 2 + j, 0)
                        for j in range(2):
                            inner_high(k, t, j)
                            if not later(k):
                                start_part(0, 4 + j)
                                high(0, 4 + j, 0)
                        for g in made:
                            start_part(pair + 1, g)
                            high(pair + 1, g, 1 - sl)

            for g in range(2):
                start_part(0, g)
                high(0, g, 0)
            body(0)
            with act.Fori(1, PAIRS // 2 - 1) as it:
                body(it)
            body(PAIRS // 2 - 1)

        @block.vector
        def _(dve):
            def merge(pair, g, sl):
                m, half = divmod(g, 2)
                if g == 0:
                    dve.wait_ge(mask_ld[sl], 8 * pair + 16 - 8 * sl)
                    dve.nop(nofuse=True)
                dve.wait_ge(start_read, GROUPS * pair + g + 1)
                dve.nop(nofuse=True)
                dve.copy_predicated(w_new[:, g % 2, :], mask[:, sl, m // 2, half * 512:(half + 1) * 512],
                                    end_bank[:, :]).then_inc(w_merged, 1)

            def low(pair, g, sl):
                m, half = divmod(g, 2)
                cols = slice(half * 512, (half + 1) * 512)
                dve.wait_ge(wh_ready, GROUPS * pair + g + 1)
                dve.tensor_tensor(w_lo[:, sl, m, cols], w_new[:, g % 2, :], w_hi[:, sl, m, cols].bitcast(F32),
                                  ALU.subtract).then_inc(wl_ready, 1)

            def multiply(k, t, j):
                dve.wait_ge(silu_ready, 2 * k + j + 1)
                dve.wait_ge(up_full, 2 * k + j + 1)
                if later(k):
                    dve.wait_ge(il_ready, 2 * k + j - 1)
                dve.tensor_tensor(inner[:, j, :], up_bank[j][:, :], silu[:, j, :], ALU.mult
                                  ).then_inc(inner_ready, 1)

            def add_down(pair, t, tiles):
                k = 4 * pair + t
                if not later(pair) and tiles[0] == 0:
                    dve.wait_ge(acc_ld[t], 16 * QT)
                    dve.wait_ge(bo_added, QT * (t + 1))
                for i in tiles:
                    at = acc[:, QT * t + i, :]
                    dve.wait_ge(down_full, QT * k + i + 1)
                    dve.tensor_tensor(at, down_bank[i % 2][:, :], at, ALU.add).then_inc(down_added, 1)

            def body(it):
                for sl in range(2):
                    pair = 2 * it + sl
                    for t in range(B):
                        k = 4 * pair + t
                        made = WGEN[t] if not last(pair) else ()
                        if not later(k):
                            for g in (2, 3):
                                merge(0, g, 0)
                                low(0, g, 0)
                        for j in range(2):
                            multiply(k, t, j)
                            if not later(k):
                                merge(0, 4 + j, 0)
                                low(0, 4 + j, 0)
                        done = (pair, t - 1) if t else (pair - 1, B - 1)
                        for g in made[:1]:
                            merge(pair + 1, g, 1 - sl)
                        if later(k):
                            add_down(*done, (0,))
                        for g in made[:1]:
                            low(pair + 1, g, 1 - sl)
                        if later(k):
                            add_down(*done, (1, 2, 3))
                        for g in made[1:]:
                            merge(pair + 1, g, 1 - sl)
                            low(pair + 1, g, 1 - sl)

            for g in range(2):
                merge(0, g, 0)
                low(0, g, 0)
            body(0)
            with dve.Fori(1, PAIRS // 2 - 1) as it:
                body(it)
            body(PAIRS // 2 - 1)
            add_down(PAIRS - 1, B - 1, range(QT))

        @block.gpsimd
        def _(pool):
            def inner_low(k, t, j):
                pool.wait_ge(ih_ready, 2 * k + j + 1)
                if not isinstance(k, int) or k >= 2:
                    pool.wait_ge(down_full, QT * (k - 1))
                pool.tensor_tensor(in_lo[:, t % 2, j, :], inner[:, j, :], in_hi[:, t % 2, j, :].bitcast(F32),
                                   ALU.subtract).then_inc(il_ready, 1)

            def body(it):
                for sl in range(2):
                    pair = 2 * it + sl
                    for t in range(B):
                        for j in range(2):
                            inner_low(4 * pair + t, t, j)
                        if isinstance(pair, int) and pair == 0:
                            pool.wait_ge(bo_ld, 16)
                            pool.wait_ge(acc_ld[t], 16 * QT)
                            for i in range(QT):
                                at = acc[:, QT * t + i, :]
                                pool.tensor_tensor(at, at, bo_all[:], ALU.add).then_inc(bo_added, 1)

            body(0)
            with pool.Fori(1, PAIRS // 2) as it:
                body(it)

        @block.sync
        def _(sp):
            def load_weights(pair, sl):
                at = pair * PW
                for m in range(MATS):
                    if later(pair - 1):
                        sp.wait_ge(ends_full, GROUPS * (pair - 2) + 2 * (m + 1))
                        sp.nop(nofuse=True)
                    for e, row in ((0, 0), (1, END_ROW)):
                        src = coef_d[e, :, m, at:at + PW] if isinstance(at, int) else \
                            coef_d[e, :, m, bass.ds(at, PW)]
                        sp.dma_start(coef[row:row + KPOLY, sl, m, :].bitcast(F32), src
                                     ).then_inc(coef_ld[sl][m], 16)
                if isinstance(pair, int):
                    src = c_mask[pair]
                else:
                    src = c_mask[bass.ds(pair, 1)].rearrange("a p k n -> (a p) k n")
                if later(pair - 1):
                    sp.wait_ge(w_merged, GROUPS * (pair - 1))
                    sp.nop(nofuse=True)
                sp.dma_start(mask[:, sl].bitcast(U32), src).then_inc(mask_ld[sl], 16)

            def body(it):
                for sl in range(2):
                    load_weights(2 * it + sl + 2, sl)

            load_weights(0, 0)
            for b in range(B):
                sp.dma_start(xt[:, b].rearrange("p e c n -> p e (c n)").bitcast(F32),
                             xt_d[2 * b:2 * b + 2].rearrange("e p n -> p e n")).then_inc(xt_ld[b], 16)
                if b == 0:
                    load_weights(1, 1)
            sp.dma_start(bo_all[:], bo.partition_broadcast(P)).then_inc(bo_ld, 16)
            for n in range(NT):
                sp.dma_start(acc[:, n, :], mid_d[n]).then_inc(acc_ld[n // QT], 16)
            body(0)
            with sp.Fori(1, PAIRS // 2 - 1) as it:
                body(it)
            for n in range(NT):
                sp.wait_ge(down_added, QT * B * (PAIRS - 1) + n + 1)
                sp.dma_start(out_t[n], acc[:, n, :]).then_inc(stored, 16)
            sp.wait_ge(stored, 16 * NT)


_INS = ["x", "Wq", "Wk", "Wv", "Wo", "bq", "bk", "bv", "bo"]


def kernel(**inputs):
    import concourse.bacc as _bacc
    from concourse.bass_utils import run_bass_kernel_spmd as _run

    nc = _bacc.Bacc("TRN2", target_bir_lowering=False, num_devices=1)
    arrays = {n: np.ascontiguousarray(inputs[f"L0_attn_{n}"]) for n in _INS}
    for n in ("Wq", "Wk", "bq", "bk"):
        w = arrays[n]
        arrays[n] = np.ascontiguousarray(w.reshape(-1, KC, HPC, HD).swapaxes(2, 3).reshape(w.shape))
    for n in ("bq", "bk"):
        arrays[n] = np.ascontiguousarray(arrays[n].reshape(KC, P).T)
    arrays["windows"] = control_windows([np.asarray(inputs[f"L0_ffn_{n}_cp"]) for n in ("gate", "up", "down")])
    arrays.update(shape_constants())
    order = [*_INS, "windows", "c_basis", "c_phase", "c_mask", "c_dist", "c_ident", "c_scale"]
    args = [nc.dram_tensor(n, arrays[n].shape, mybir.dt.from_np(arrays[n].dtype), kind="ExternalInput").ap()
            for n in order]
    result = nc.dram_tensor("result", (B, S, D), F32, kind="ExternalOutput").ap()
    build_kernel(nc, *args, result)
    r = _run(nc, [arrays], core_ids=[0])
    return r.results[0]["result"]
```

```python
from contextlib import ExitStack

import numpy as np

import concourse.bass as bass
from concourse import mybir

F32 = mybir.dt.float32
F32R = mybir.dt.float32r
F16 = mybir.dt.float16
BF16 = mybir.dt.bfloat16
U8 = mybir.dt.uint8
U32 = mybir.dt.uint32
ALU = mybir.AluOpType
ACT = mybir.ActivationFunctionType
AX_X = mybir.AxisListType.X

P = 128
B, S, D = 4, 512, 512
H, HD = 16, 32
INTER = 2048
KC = D // P
HPC = P // HD
QT = S // P
EPS = 1e-5
MASKED = -3.0e38
COMPRESSION = 128.9
N_CTRL = max(16, int(INTER * D / COMPRESSION))
MATS = 3
BLOCKS = INTER * D // P
PAIRS = INTER // (2 * P)
PW = BLOCKS // PAIRS
ROLES = 3
KPOLY = 4 * ROLES
END_ROW = 32

OFF = [0, 128, 384, 768]
PROBS = 1280


def grid():
    t = np.linspace(0.0, N_CTRL - 1.0, INTER * D, dtype=np.float64)
    seg = np.clip(np.floor(t).astype(np.int64), 0, N_CTRL - 2)
    return t, seg


def block_order():
    gate = [KC * (pr * 2 * P + i) + q for pr in range(PAIRS) for q in range(KC) for i in range(2 * P)]
    down = [(INTER // P) * o + 2 * pr + j for pr in range(PAIRS) for j in range(2) for o in range(D)]
    return np.array(gate), np.array(down)


def rounded(x):
    u = np.asarray(x, np.float32).view(np.uint32)
    return ((u + 0x7FF + ((u >> 12) & 1)) & np.uint32(0xFFFFF000)).view(np.float32)


def shape_constants():
    t, seg = grid()
    delta = (N_CTRL - 1.0) / (INTER * D - 1)
    basis = np.zeros((END_ROW + KPOLY, P), np.float32)
    for row, tau in ((0, np.arange(P) * delta), (END_ROW, (np.arange(P) - (P - 1)) * delta)):
        for d in range(4):
            hi = rounded(tau**d)
            lo = rounded(tau**d - hi)
            for role, part in enumerate((hi, lo, hi)):
                basis[row + 4 * role + d] = 0.5 * part
    phase = np.zeros((P, 2, MATS, BLOCKS // P), np.float32)
    mask = np.zeros((PAIRS, P, 2, PW), np.uint8)
    for kind, order in enumerate(block_order()):
        start, end = order * P, order * P + P - 1
        at = [t[start] - seg[start], t[end] - (seg[start] + 1)]
        for m in ((0, 1), (2,))[kind]:
            for e in range(2):
                phase[:, e, m, :] = at[e].reshape(P, -1)
        behind = seg.reshape(-1, P)[order] != seg[start][:, None]
        mask[:, :, kind, :] = behind.reshape(PAIRS, PW, P).transpose(0, 2, 1)
    key = np.arange(S)
    dist = np.broadcast_to((key - (S - 1)).astype(np.float32), (P, S)).copy()
    dist[(key[None, :] - (S - P)) > np.arange(P)[:, None]] = MASKED
    head = np.arange(P)[:, None] % HPC + HPC * np.arange(KC)
    scale = HD**-0.5 * 2.0 ** (8.0 / H * (head + 1))
    return {"c_basis": basis, "c_phase": phase, "c_mask": mask.view(np.uint32), "c_dist": dist,
            "c_ident": np.eye(P, dtype=np.float32), "c_scale": scale.astype(np.float32)}


def control_windows(points):
    _, seg = grid()
    out = []
    for order in block_order():
        first = seg[order * P]
        index = np.clip(first[None, :] + np.arange(-1, 4)[:, None], 0, N_CTRL - 1)
        out.append(index)
    rows = [points[m][out[0 if m < 2 else 1]] for m in range(MATS)]
    return np.ascontiguousarray(np.stack(rows).reshape(MATS, 5, P, -1).transpose(2, 1, 0, 3))


def later(b):
    return not isinstance(b, int) or b > 0


def rows_of(ap, index):
    if isinstance(index, int):
        return ap[index]
    return ap[bass.ds(index, 1)].rearrange("a p n -> (a p) n")


def build_kernel(nc, x, wq, wk, wv, wo, bq, bk, bv, bo, win, c_basis, c_phase, c_mask, c_dist, c_ident, c_scale, out):
    coef_d = nc.dram_tensor("coef_scratch", (2, KPOLY, MATS, BLOCKS), F32, kind="Internal").ap()
    xt_d = nc.dram_tensor("xt_scratch", (B * 2, P, KC * S), F32, kind="Internal").ap()
    mid_d = nc.dram_tensor("mid_scratch", (B * QT, P, D), F32, kind="Internal").ap()
    x_t = x.rearrange("b (t p) d -> (b t) p d", p=P)
    out_t = out.rearrange("b (t p) d -> (b t) p d", p=P)

    with ExitStack() as outer:
        def sems(ctx, *names):
            return [ctx.enter_context(nc.semaphore(n)) for n in names]

        psum = [outer.enter_context(nc.psum_tensor(f"bank{i}", [P, 512], F32)) for i in range(8)]
        basis = outer.enter_context(nc.sbuf_tensor("basis", [END_ROW + KPOLY, P], F32R))
        w_room = outer.enter_context(nc.sbuf_tensor("w_room", [P, 2, 4, KC, D], F32R))
        coef = w_room[0:END_ROW + KPOLY, 0, 0:3].rearrange("p a c n -> p (a c n)").rearrange(
            "p (s m n) -> p s m n", s=2, m=MATS)
        xt_room = outer.enter_context(nc.sbuf_tensor("xt_room", [P, 2, KC, S], F32R))
        v_room = outer.enter_context(nc.sbuf_tensor("v_room", [P, QT, D], F32))
        mask = v_room[:, 0:2].rearrange("p a n -> p (a n)").bitcast(U8).rearrange("p (s k n) -> p s k n", s=2, k=2)
        res_st = sems(outer, *[f"res_st{t}" for t in range(QT)])
        xt_st, = sems(outer, "xt_st")
        stored = (res_st, xt_st)
        coef_ld = [sems(outer, *[f"coef_ld{sl}_{m}" for m in range(MATS)]) for sl in range(2)]
        mask_ld = sems(outer, "mask_ld0", "mask_ld1")

        def load_coef(sp, pair, sl, m):
            at = pair * PW
            for e, row in ((0, 0), (1, END_ROW)):
                src = coef_d[e, :, m, at:at + PW] if isinstance(at, int) else coef_d[e, :, m, bass.ds(at, PW)]
                sp.dma_start(coef[row:row + KPOLY, sl, m, :].bitcast(F32), src).then_inc(coef_ld[sl][m], 16)

        def load_mask(sp, pair, sl):
            src = c_mask[pair] if isinstance(pair, int) else \
                c_mask[bass.ds(pair, 1)].rearrange("a p k n -> (a p) k n")
            sp.dma_start(mask[:, sl].bitcast(U32), src).then_inc(mask_ld[sl], 16)

        attention(nc, sems, psum, basis, w_room, v_room, xt_room, stored, load_coef, load_mask,
                  (wq, wk, wv, wo), bq, bk, bv, win, c_basis, c_phase, c_dist, c_ident, c_scale, coef_d, x_t,
                  xt_d, mid_d)
        ffn(nc, sems, psum, basis, w_room, v_room, xt_room, stored, coef, mask, coef_ld, mask_ld, load_coef,
            load_mask, xt_d, mid_d, bo, out_t)


HALF = H // 2
UNITS = {0: [("q", 1)], 1: [("k", 1)], 2: [("o", 0)], 3: [("o", 1)], 4: [("q", 2)], 5: [("k", 2)], 6: [("o", 2)],
         7: [("o", 3)], 8: [("q", 3)], 9: [("k", 3)], 11: [("v", 0), ("v", 1)], 12: [("q", 0)],
         13: [("k", 0)], 14: [("v", 2)], 15: [("v", 3)]}
TURNS = {2: [("c", 3)], 7: [("c", 0)], 9: [("x", 0), ("x", 1)], 10: [("x", 2), ("x", 3)], 11: [("c", 1)],
         15: [("c", 2)]}


SPLITS = {13: [(0, 0)], 14: [(0, 1)], 1: [(0, 2)], 2: [(0, 3)], 4: [(1, 0)], 5: [(1, 1)], 6: [(1, 2)], 7: [(1, 3)]}


def slope(h):
    return 2.0 ** (-8.0 / H * (h + 1))


def place(key, s):
    kind, n = key
    if s < HALF:
        return -1 if kind == "o" or key == ("c", 3) else 0
    return 1 if kind in "xv" or (kind in "qk" and n == 0) else 0


def steps_keys(steps, before=True):
    return [key for s in steps for key in UNITS.get(s, []) + TURNS.get(s, []) if before or place(key, s) == 0]


W_PIECES = 8
STACK = 16 * ROLES


PJ_FIRST = [("x", t) for t in range(QT)] + [("q", 0), ("k", 0), ("v", 0), ("v", 1), ("v", 2), ("q", 1), ("v", 3),
                                            ("k", 1)] + steps_keys(range(2, HALF), before=False)
PJ_BODY = steps_keys([*range(HALF, H), *range(HALF)])
PJ_BODY_ENDS = list(PJ_BODY)
PJ_BODY_ENDS.remove(("o", 0))
PJ_BODY_ENDS.insert(PJ_BODY_ENDS.index(("c", 3)) + 1, ("o", 0))
PJ_LAST = [("q", 3), ("k", 3), ("c", 1), ("c", 2), ("o", 0), ("o", 1), ("c", 3), ("o", 2), ("o", 3)]
PJ_LAST_ENDS = [("q", 3), ("k", 3), ("c", 1), ("c", 2), ("c", 3)] + [("o", t) for t in range(QT)]
CARRIED = [("q", 3), ("k", 3)] + [("c", c) for c in range(1, KC)] + [("o", t) for t in range(QT)]


def pj_before(key, b, body=PJ_BODY, at_end=PJ_LAST):
    if not later(b) and key in PJ_FIRST:
        return 0, PJ_FIRST.index(key)
    n = body.index(key)
    if key in CARRIED and isinstance(b, int) and b == B - 1:
        n = at_end.index(key)
    return (b if key in CARRIED else b - 1), len(PJ_FIRST) + n


def pj_use(key, b):
    times, rest = pj_before(key, b)
    return rest % 3, times * (len(PJ_BODY) // 3) + rest // 3


def pj_total(key, b):
    times, rest = pj_before(key, b, PJ_BODY_ENDS, PJ_LAST_ENDS)
    return times * len(PJ_BODY) + rest + 1


def back(b, s, n):
    if s - n >= H:
        return None
    if s - n >= 0:
        return b, s - n
    return (b - 1, s - n + H) if later(b) else None


def active(table, s, carry):
    return [key for key in table.get(s, []) if carry or place(key, s) == 0]


def attention(nc, sems, psum, basis, w_room, v_room, xt_room, stored, load_coef, load_mask, weights, bq, bk, bv,
              win, c_basis, c_phase, c_dist, c_ident, c_scale,
              coef_d, x_t, xt_d, mid_d):
    NB = BLOCKS // P
    with ExitStack() as ctx:
        sb = lambda n, s, dt: ctx.enter_context(nc.sbuf_tensor(n, s, dt))
        w_hi, w_lo = w_room[:, 0], w_room[:, 1]
        dist = sb("dist", [P, S], F32)
        ident = sb("ident", [P, P], F32)
        ident16 = sb("ident16", [P, P], F16)
        bv_all = sb("bv_all", [P, D], F32)
        b_qk = sb("b_qk", [P, 2, KC], F32)
        q_scale = sb("q_scale", [P, KC], F32)
        b_scaled = sb("b_scaled", [P, KC], F32)
        x_in = sb("x_in", [P, QT, D], F32)
        xt_hi, xt_lo = xt_room[:, 0], xt_room[:, 1]
        warm = sb("warm", [1, 1], F32)
        qk_full = sb("qk_full", [P, S], F32)
        parts = sb("parts", [P, 4, S], F32R)
        q_stack = sb("q_stack", [3 * HD, 2, HPC, S], F32R)
        k_stack = sb("k_stack", [3 * HD, 2, HPC, S], F32R)
        v_full = v_room
        v_parts = sb("v_parts", [P, QT, H, 3, HD], BF16)
        ctx_tmp = sb("ctx_tmp", [P, 2, QT, HD], F32)
        stats = sb("stats", [P, QT, 6], F32)
        meanvar = sb("meanvar", [P, QT, 2], F32)
        varp = sb("varp", [P, QT], F32)
        rstd = sb("rstd", [P, QT], F32)
        minus_half = sb("minus_half", [P, QT], F32)
        row_max = sb("row_max", [P, 2, QT], F32)
        neg_max = sb("neg_max", [P, 2, QT], F32)
        row_sum = sb("row_sum", [P, 4, QT], F32)
        inv_sum = sb("inv_sum", [P, 2, QT], F32)
        work = sb("work", [P, 3 * 2 * PROBS], F32)
        probs = work[:, 0:2 * PROBS].rearrange("p (s n) -> p s n", s=2)
        probs16 = work[:, 2 * PROBS:4 * PROBS].bitcast(F16).rearrange("p (s e n) -> p s e n", s=2, e=2)
        probs_t = work[:, 4 * PROBS:6 * PROBS].bitcast(F16).rearrange("p (s n) -> p s n", s=2)
        at = 3 * 2 * D
        w_raw = work[:, 0:at].rearrange("p (s c n) -> p s c n", s=3, c=2)
        points = work[:, at:at + 5 * MATS * NB].rearrange("p (k n) -> p k n", k=5)
        at += 5 * MATS * NB
        phase = work[:, at:at + 2 * MATS * NB].rearrange("p (e n) -> p e n", e=2)
        at += 2 * MATS * NB
        tmp = work[:, at:at + 8 * MATS * NB].rearrange("p (k e n) -> p k e n", k=4, e=2)
        at += 8 * MATS * NB
        poly = work[:, at:at + 8 * MATS * NB].rearrange("p (d e n) -> p d e n", d=4, e=2)
        basis_raw = ctx_tmp[0:END_ROW + KPOLY].rearrange("p a q d -> p (a q d)")[:, 0:P]
        ctx_sb = sb("ctx_sb", [P, 2, QT, P], F32)
        ctx_t = sb("ctx_t", [P, 2, KC, S], F32R)
        poly_hi, poly_lo = [ctx_t[:, e].rearrange("p c n -> p (c n)")[:, 0:8 * MATS * NB]
                            .rearrange("p (d e m n) -> p d e m n", d=4, e=2, m=MATS) for e in range(2)]

        pj_bank, score_bank, av_bank = [psum[0], psum[1], psum[6]], psum[2:4], psum[7]
        pt_bank = [p[:, :].bitcast(F16) for p in psum[4:6]]

        x_ld = sems(ctx, *[f"x_ld{t}" for t in range(QT)])
        w_ld = sems(ctx, "w_ld0", "w_ld1", "w_ld2")
        pj_free = sems(ctx, "pj_free0", "pj_free1", "pj_free2")
        pt_free = sems(ctx, "pt_free0", "pt_free1")
        stacked = [sems(ctx, f"{m}_stacked0", f"{m}_stacked1") for m in "qk"]
        res_ld = sems(ctx, *[f"res_ld{t}" for t in range(QT)])
        res_st, xt_st = stored
        (ident_ld, const_ld, points_ld, wh_ready, wl_ready, wl_pool, small_set, poly_step, ph_ready, pl_ready, coef_st,
         pj_full, ln_stats, ln_mv, ln_var, rstd_ready, xn_ready, xh_ready,
         full_ready, ql_ready, v_rest, v_mid, vh_ready, v_done, s_full, t_done, nm_ready, p_ready, hi_ready,
         lo_ready, pt_full, av_full, av_read, ctx_ready, ch_ready) = sems(
            ctx, "ident_ld", "const_ld", "points_ld", "wh_ready", "wl_ready", "wl_pool", "small_set", "poly_step",
            "ph_ready", "pl_ready", "coef_st", "pj_full", "ln_stats", "ln_mv",
            "ln_var", "rstd_ready", "xn_ready", "xh_ready", "full_ready", "ql_ready", "v_rest", "v_mid",
            "vh_ready", "v_done", "s_full", "t_done", "nm_ready", "p_ready", "p_hi_ready", "p_lo_ready",
            "pt_full", "av_full", "av_read", "ctx_ready", "ch_ready")

        block = ctx.enter_context(nc.Block())

        def w_piece(w, n):
            m, half = divmod(n, 2)
            return w[:, m, 2 * half:2 * half + 2, :]

        @block.tensor
        def _(pe):
            def turn_x(b, t):
                bank, used = pj_use(("x", t), b)
                if later(b) or used:
                    pe.wait_ge(pj_free[bank], used)
                pe.wait_ge(xn_ready, QT * b + t + 1)
                if not later(b) and t == 0:
                    pe.wait_ge(ident_ld, 16)
                for c in range(KC):
                    mm = pe.transpose(pj_bank[bank][:, c * P:(c + 1) * P], x_in[:, t, c * P:(c + 1) * P],
                                      ident[:])
                mm.then_inc(pj_full, 1)

            def product(bank, pairs, some):
                n = len(pairs)
                mm = None
                for k in some:
                    l_hi, l_lo, r_hi, r_lo = pairs[k]
                    pe.matmul(bank[:, :], l_hi, r_hi, start=(k == 0), stop=False)
                    pe.matmul(bank[:, :], l_hi, r_lo, start=False, stop=False)
                    mm = pe.matmul(bank[:, :], l_lo, r_hi, start=False, stop=(k == n - 1))
                if some[-1] == n - 1:
                    mm.then_inc(pj_full, 1)

            def project_qk(b, name, c, some=(0, 1, 2, 3)):
                bank, used = pj_use((name, c), b)
                m = "qk".index(name)
                if some[0] == 0:
                    pe.wait_ge(pj_free[bank], used)
                    if c == 0 and m == 0:
                        x_bank, x_used = pj_use(("x", QT - 1), b)
                        pe.wait_ge(pj_free[x_bank], x_used + 1)
                if not later(b) and c == 0:
                    pe.wait_ge(wl_ready, 2 * m + 2)
                cols = slice(c * P, (c + 1) * P)
                product(pj_bank[bank], [(w_hi[:, m, k, cols], w_lo[:, m, k, cols], xt_hi[:, k, :],
                                         xt_lo[:, k, :]) for k in range(KC)], some)

            def project_v(b, t, some=(0, 1, 2, 3)):
                bank, used = pj_use(("v", t), b)
                if some[0] == 0:
                    pe.wait_ge(pj_free[bank], used)
                    x_bank, x_used = pj_use(("x", t), b)
                    pe.wait_ge(pj_free[x_bank], x_used + 1)
                if not later(b) and t == 0 and some[0] == 0:
                    pe.wait_ge(wl_pool, 2)
                rows = slice(t * P, (t + 1) * P)
                product(pj_bank[bank], [(xt_hi[:, k, rows], xt_lo[:, k, rows], w_hi[:, 2, k, :],
                                         w_lo[:, 2, k, :]) for k in range(KC)], some)

            def scores(b, s, i):
                c, h = divmod(s, HPC)
                if h == 0 and i == 0:
                    pe.wait_ge(stacked[0][c % 2], 2 * STACK * b + STACK * (c // 2 + 1))
                    pe.wait_ge(stacked[1][c % 2], 2 * STACK * b + STACK * (c // 2 + 1))
                if later(b) or 4 * s + i >= 2:
                    pe.wait_ge(t_done, 64 * b + 4 * s + i - 1)
                n = max(2, i + 1) * P
                pe.matmul(score_bank[i % 2][:, 0:n], q_stack[:, c % 2, h, i * P:(i + 1) * P],
                          k_stack[:, c % 2, h, 0:n], start=True, stop=True).then_inc(s_full, 1)

            def turn_probs(b, s, i):
                if i == 0:
                    if not later(b) and s == 0:
                        pe.wait_ge(small_set, 2)
                    pe.wait_ge(hi_ready, H * b + s + 1)
                    pe.wait_ge(lo_ready, H * b + s + 1)
                if later(b) or 2 * s + i // 2 > 0:
                    pe.wait_ge(pt_free[i % 2], 2 * (H * b + s) + i // 2)
                n = i + 1
                for part in range(2):
                    for k in range(n):
                        mm = pe.transpose(pt_bank[i % 2][:, (part * n + k) * P:(part * n + k + 1) * P],
                                          probs16[:, s % 2, part, OFF[i] + k * P:OFF[i] + (k + 1) * P],
                                          ident16[:])
                mm.then_inc(pt_full, 1)

            def weigh_values(b, s, i):
                if i == 0:
                    if later(b) or s >= 1:
                        pe.wait_ge(av_read, H * b + s)
                    if s % HALF == 0:
                        pe.wait_ge(v_done, 2 * QT * b + QT * (s // HALF + 1))
                bank = av_bank
                pe.wait_ge(pt_free[i % 2], 2 * (H * b + s) + i // 2 + 1)
                n = i + 1
                for k in range(n):
                    at = 2 * OFF[i] + k * P
                    pe.matmul(bank[:, i * 96:(i + 1) * 96], probs_t[:, s % 2, at:at + P],
                              v_parts[:, k, s, :, :], start=(k == 0), stop=False)
                    at += n * P
                    mm = pe.matmul(bank[:, i * 96:i * 96 + 64], probs_t[:, s % 2, at:at + P],
                                   v_parts[:, k, s, 0:2, :], start=False, stop=(k == n - 1))
                if i == QT - 1:
                    mm.then_inc(av_full, 1)

            def turn_ctx(b, c):
                bank, used = pj_use(("c", c), b)
                pe.wait_ge(pj_free[bank], used)
                pe.wait_ge(ctx_ready, H * b + HPC * (c + 1))
                for q in range(QT):
                    mm = pe.transpose(pj_bank[bank][:, q * P:(q + 1) * P], ctx_sb[:, c % 2, q, :], ident[:])
                mm.then_inc(pj_full, 1)

            def project_out(b, q, some=(0, 1, 2, 3)):
                bank, used = pj_use(("o", q), b)
                if q == 0:
                    c_bank, c_used = pj_use(("c", max(some) if len(some) < KC else KC - 1), b)
                if some[0] == 0:
                    pe.wait_ge(pj_free[bank], used)
                if q == 0:
                    pe.wait_ge(pj_free[c_bank], c_used + 1)
                if some[0] == 0:
                    if q == 0:
                        if not later(b):
                            pe.wait_ge(wl_pool, 4)
                rows = slice(q * P, (q + 1) * P)
                product(pj_bank[bank], [(ctx_t[:, 0, c, rows], ctx_t[:, 1, c, rows],
                                         w_hi[:, 3, c, :], w_lo[:, 3, c, :]) for c in range(KC)], some)

            def unit(b, s, key, some=(0, 1, 2, 3)):
                of, (kind, n) = b + place(key, s), key
                if kind in "qk":
                    project_qk(of, kind, n, some)
                elif kind == "v":
                    project_v(of, n, some)
                else:
                    project_out(of, n, some)

            def step(b, s, carry):
                own, turned, weighed = back(b, s, 0), back(b, s, 2), back(b, s, 3)
                units, turns = active(UNITS, s, carry), active(TURNS, s, carry)
                early, rest = ([], units) if s == 3 else (units[:1], units[1:])
                for i in range(2):
                    if own:
                        scores(b, s, i)
                for i in range(2):
                    if weighed:
                        weigh_values(*weighed, i)
                for key in early:
                    unit(b, s, key, (0, 1))
                for i in range(2, QT):
                    if own:
                        scores(b, s, i)
                if turned:
                    turn_probs(*turned, 0)
                for key in early:
                    unit(b, s, key, (2,))
                if turned:
                    turn_probs(*turned, 1)
                for i in range(2, QT):
                    if weighed:
                        weigh_values(*weighed, i)
                for key in early if s != 2 else []:
                    unit(b, s, key, (3,))
                for i in range(2, QT):
                    if turned:
                        turn_probs(*turned, i)
                if s == 3 and carry:
                    project_out(b - 1, 0, (3,))
                for key in rest:
                    unit(b, s, key)
                for key in turns:
                    (turn_x if key[0] == "x" else turn_ctx)(b + place(key, s), key[1])

            for t in range(QT):
                turn_x(0, t)
            project_qk(0, "q", 0)
            project_qk(0, "k", 0)
            for t in range(3):
                project_v(0, t)
            for s in range(HALF):
                step(0, s, False)
                if s == 0:
                    project_v(0, 3)
            with pe.Fori(1, B) as b:
                for s in range(HALF, H):
                    step(b - 1, s, True)
                for s in range(HALF):
                    step(b, s, True)
            for s in range(HALF, H + 3):
                step(B - 1, s, False)
                if s > H:
                    project_out(B - 1, s - H - 1, (0, 1, 2))
            turn_ctx(B - 1, KC - 1)
            for q in range(2):
                project_out(B - 1, q, (3,))
            for q in range(2, QT):
                project_out(B - 1, q)

        @block.vector
        def _(dve):
            def norm_stats(b, tiles):
                for t in tiles:
                    dve.wait_ge(x_ld[t], 16 * b + 16)
                    dve.bn_stats(stats[:, t, :], x_in[:, t, :]).then_inc(ln_stats, 1)
                dve.wait_ge(ln_stats, QT * b + tiles[-1] + 1)
                dve.nop(nofuse=True)
                for t in tiles:
                    dve.bn_aggr(meanvar[:, t, :], stats[:, t, :]).then_inc(ln_mv, 1)
                dve.wait_ge(ln_mv, QT * b + tiles[-1] + 1)
                two = slice(tiles[0], tiles[-1] + 1)
                dve.tensor_scalar(varp[:, two], meanvar[:, two, 1], EPS, None, ALU.add).then_inc(ln_var, 1)

            def norm_apply(b, t):
                if t % 2 == 0:
                    dve.wait_ge(rstd_ready, 2 * b + t // 2 + 1)
                dve.tensor_scalar(x_in[:, t, :], x_in[:, t, :], meanvar[:, t, 0:1], rstd[:, t:t + 1],
                                  ALU.subtract, ALU.mult).then_inc(xn_ready, 1)

            def x_low(b, t):
                bank, _ = pj_use(("x", t), b)
                rows = slice(t * P, (t + 1) * P)
                dve.wait_ge(xh_ready, QT * b + t + 1)
                if later(b) and t == 0:
                    dve.wait_ge(xt_st, 32 * b)
                dve.tensor_tensor(xt_lo[:, :, rows], pj_bank[bank][:, :].rearrange("p (c n) -> p c n", c=KC),
                                  xt_hi[:, :, rows].bitcast(F32), ALU.subtract).then_inc(pj_free[bank], 1)

            def v_take(b, t):
                bank, _ = pj_use(("v", t), b)
                dve.wait_ge(pj_full, pj_total(("v", t), b))
                if later(b) and t == 0:
                    dve.wait_ge(v_done, 2 * QT * b)
                dve.tensor_tensor(v_full[:, t, :], pj_bank[bank][:, :], bv_all[:], ALU.add
                                  ).then_inc(pj_free[bank], 1)

            def v_split(b, half, t):
                heads = slice(half * HALF, (half + 1) * HALF)
                full = v_full[:, t, :].rearrange("p (h d) -> p h d", h=H)[:, heads]
                n = 2 * QT * b + QT * half + t + 1
                dve.wait_ge(vh_ready, n)
                dve.tensor_tensor(full, full, v_parts[:, t, heads, 0, :], ALU.subtract).then_inc(v_rest, 1)
                dve.wait_ge(v_rest, n)
                dve.tensor_copy(v_parts[:, t, heads, 1, :], full).then_inc(v_mid, 1)
                dve.wait_ge(v_mid, n)
                dve.tensor_tensor(v_parts[:, t, heads, 2, :], full, v_parts[:, t, heads, 1, :],
                                  ALU.subtract).then_inc(v_done, 1)

            def bias_and_max(b, s, tiles):
                if (later(b) or s >= 2) and tiles[0] == 0:
                    dve.wait_ge(lo_ready, H * b + s - 1)
                for i in tiles:
                    n = (i + 1) * P
                    dve.wait_ge(s_full, 64 * b + 4 * s + i + 1)
                    dve.nop(nofuse=True)
                    dve.tensor_tensor_reduce(
                        probs[:, s % 2, OFF[i]:OFF[i] + n], score_bank[i % 2][:, 0:n], dist[:, S - n:S],
                        1.0, -3.4e38, ALU.add, ALU.max, row_max[:, s % 2, i:i + 1]).then_inc(t_done, 1)

            def negate_max(b, s):
                dve.wait_ge(t_done, 64 * b + 4 * s + 4)
                dve.tensor_scalar(neg_max[:, s % 2, :], row_max[:, s % 2, :], -slope(s), None,
                                  ALU.mult).then_inc(nm_ready, 1)

            def probs_high(b, s):
                dve.wait_ge(p_ready, H * b + s + 1)
                if later(b) or s >= 2:
                    dve.wait_ge(pt_full, 4 * (H * b + s - 1))
                dve.tensor_copy(probs16[:, s % 2, 0, :], probs[:, s % 2, :]).then_inc(hi_ready, 1)

            def take_turned(b, s, i):
                n = 2 * (i + 1) * P
                dve.wait_ge(pt_full, 4 * (H * b + s) + i + 1)
                if i == 0 and (later(b) or s >= 2):
                    dve.wait_ge(av_full, H * b + s - 1)
                dve.tensor_copy(probs_t[:, s % 2, 2 * OFF[i]:2 * OFF[i] + n],
                                pt_bank[i % 2][:, 0:n]).then_inc(pt_free[i % 2], 1)

            def normalize(b, s):
                c, h = divmod(s, HPC)
                dve.wait_ge(av_full, H * b + s + 1)
                if later(b) or s >= 2:
                    dve.wait_ge(ctx_ready, H * b + s - 1)
                dve.reciprocal(inv_sum[:, s % 2, :], row_sum[:, s % 4, :])
                dve.tensor_reduce(ctx_tmp[:, s % 2],
                                  av_bank[:, 0:QT * 96].rearrange("p (q t d) -> p q d t", q=QT, t=3),
                                  AX_X, ALU.add).then_inc(av_read, 1)
                dve.wait_ge(av_read, H * b + s + 1)
                if h == 0 and (later(b) or c >= 2):
                    dve.wait_ge(pj_full, pj_total(("c", (c - 2) % KC), b if c >= 2 else b - 1))
                dve.tensor_tensor(ctx_sb[:, c % 2, :, h * HD:(h + 1) * HD], ctx_tmp[:, s % 2],
                                  inv_sum[:, s % 2, :].unsqueeze(2).broadcast_to([P, QT, HD]),
                                  ALU.mult).then_inc(ctx_ready, 1)

            def ctx_low(b, c):
                bank, _ = pj_use(("c", c), b)
                dve.wait_ge(ch_ready, KC * b + c + 1)
                dve.tensor_tensor(ctx_t[:, 1, c, :], pj_bank[bank][:, :], ctx_t[:, 0, c, :].bitcast(F32),
                                  ALU.subtract).then_inc(pj_free[bank], 1)

            def add_residual(b, q):
                bank, _ = pj_use(("o", q), b)
                dve.wait_ge(pj_full, pj_total(("o", q), b))
                dve.wait_ge(res_ld[q], 16 * b + 16)
                dve.tensor_tensor(x_in[:, q, :], pj_bank[bank][:, :], x_in[:, q, :], ALU.add
                                  ).then_inc(pj_free[bank], 1)

            def step(b, s, carry, carried):
                halved, turned, weighed = back(b, s, 1), back(b, s, 2), back(b, s, 3)
                last = (s - 1) % H
                before = b - 1 if s == 0 else b
                if s > H or (s == 0 and not later(b)):
                    units = turns = []
                else:
                    units = [(before + place(key, last), key) for key in active(UNITS, last, carried)]
                    turns = [(before + place(key, last), key) for key in active(TURNS, last, carried)]
                if s < H:
                    bias_and_max(b, s, (0, 1))
                for of, (kind, n) in units:
                    if kind == "v":
                        v_take(of, n)
                    elif kind == "o" and n > 0:
                        add_residual(of, n)
                if not later(b) and s in (0, 1):
                    v_take(b, s + 2)
                if halved:
                    probs_high(*halved)
                if s < H:
                    bias_and_max(b, s, (2, 3))
                    negate_max(b, s)
                if not later(b) and s == 0:
                    v_split(b, 0, 0)
                    v_split(b, 0, 1)
                if not later(b) and s == 2:
                    dve.wait_ge(pl_ready, 1)
                if s == 3:
                    for of, (_, c) in turns:
                        ctx_low(of, c)
                if turned:
                    take_turned(*turned, 0)
                    take_turned(*turned, 1)
                if weighed:
                    normalize(*weighed)
                if carry and s == 9:
                    norm_apply(b + 1, 0)
                    norm_apply(b + 1, 1)
                if carry and s == 10:
                    norm_apply(b + 1, 2)
                    norm_apply(b + 1, 3)
                for of, (kind, n) in turns if s != 3 else []:
                    (x_low if kind == "x" else ctx_low)(of, n)
                if carry and s == 3:
                    add_residual(b - 1, 0)
                if carry and s == HALF - 1:
                    add_residual(b - 1, QT - 1)
                if carry and s in (8, 9):
                    norm_stats(b + 1, (2 * s - 16, 2 * s - 15))
                for half, t in SPLITS.get(s, []):
                    if s >= HALF:
                        if carry:
                            v_split(b + 1, half, t)
                    else:
                        v_split(b, half, t)

            def w_low(n):
                dve.wait_ge(wh_ready, n + 1)
                dve.tensor_tensor(w_piece(w_lo, n), w_raw[:, n % 3], w_piece(w_hi, n).bitcast(F32),
                                  ALU.subtract).then_inc(wl_ready, 1)

            steps = [0]

            def then(ins):
                steps[0] += 1
                ins.then_inc(poly_step, 1)
                dve.wait_ge(poly_step, steps[0])

            def polynomials(part):
                p0, p1, p2, p3 = [points[:, k:k + 2, :] for k in range(4)]
                c1, c2, u, v = [tmp[:, k] for k in range(4)]
                a0, a1, a2, a3 = [poly[:, d] for d in range(4)]
                if part == 1:
                    then(dve.tensor_tensor(a1, a2, phase, ALU.mult))
                    then(dve.tensor_tensor(a1, a1, c1, ALU.add))
                    then(dve.tensor_tensor(a0, a1, phase, ALU.mult))
                    dve.scalar_tensor_tensor(a0, p1, 2.0, a0, ALU.mult, ALU.add)
                    then(dve.tensor_tensor(a2, a2, v, ALU.add))
                    then(dve.tensor_tensor(u, a2, phase, ALU.mult))
                    dve.tensor_tensor(a2, a2, v, ALU.add)
                    then(dve.tensor_tensor(a1, a1, u, ALU.add))
                    return
                dve.wait_ge(points_ld, 32 + 16)
                dve.tensor_tensor(c1, p2, p0, ALU.subtract)
                dve.tensor_tensor(u, p3, p0, ALU.subtract)
                then(dve.tensor_tensor(v, p1, p2, ALU.subtract))
                dve.scalar_tensor_tensor(a3, v, 3.0, u, ALU.mult, ALU.add)
                then(dve.scalar_tensor_tensor(c2, p0, 2.0, p3, ALU.mult, ALU.subtract))
                then(dve.scalar_tensor_tensor(c2, p1, -5.0, c2, ALU.mult, ALU.add))
                dve.tensor_tensor(v, a3, phase, ALU.mult)
                then(dve.scalar_tensor_tensor(c2, p2, 4.0, c2, ALU.mult, ALU.add))
                then(dve.tensor_tensor(a2, v, c2, ALU.add))

            dve.memset(minus_half[:], -0.5).then_inc(small_set, 1)
            norm_stats(0, (0, 1))
            norm_stats(0, (2, 3))
            for t in range(QT):
                norm_apply(0, t)
            w_low(0)
            x_low(0, 0)
            x_low(0, 1)
            w_low(1)
            x_low(0, 2)
            x_low(0, 3)
            dve.wait_ge(ident_ld, 16)
            dve.wait_ge(const_ld, 16 * 5)
            dve.tensor_copy(ident16[:], ident[:]).then_inc(small_set, 1)
            dve.tensor_tensor(b_scaled[:], b_qk[:, 0, :], q_scale[:], ALU.mult).then_inc(small_set, 1)
            w_low(2)
            w_low(3)
            polynomials(0)
            bank, used = pj_use(("q", 0), 0)
            dve.wait_ge(pj_free[bank], used + 1)
            dve.tensor_tensor(parts[:, 1, :], qk_full[:], parts[:, 0, :].bitcast(F32), ALU.subtract
                              ).then_inc(ql_ready, 1)
            polynomials(1)
            for t in range(2):
                v_take(0, t)
            dve.wait_ge(wl_pool, 4)
            dve.wait_ge(wl_ready, 4)
            for s in range(HALF):
                step(0, s, False, False)
            with dve.Fori(1, B) as b:
                for s in range(HALF, H):
                    step(b - 1, s, True, s > HALF)
                for s in range(HALF):
                    step(b, s, True, True)
            for s in range(HALF, H + 3):
                step(B - 1, s, False, False)
            ctx_low(B - 1, KC - 1)
            for q in range(QT):
                add_residual(B - 1, q)

        @block.scalar
        def _(act):
            def x_high(b, t):
                bank, _ = pj_use(("x", t), b)
                act.wait_ge(pj_full, pj_total(("x", t), b))
                if later(b) and t == 0:
                    act.wait_ge(xt_st, 32 * b)
                act.copy(xt_hi[:, :, t * P:(t + 1) * P],
                         pj_bank[bank][:, :].rearrange("p (c n) -> p c n", c=KC)).then_inc(xh_ready, 1)

            def qk_high(b, name, c):
                m = "qk".index(name)
                bank, _ = pj_use((name, c), b)
                scale = q_scale[:, c:c + 1] if m == 0 else 1.0
                bias = b_scaled[:, c:c + 1] if m == 0 else b_qk[:, 1, c:c + 1]
                act.wait_ge(pj_full, pj_total((name, c), b))
                if later(b) or c > 0 or m > 0:
                    act.wait_ge(ql_ready, 8 * b + 2 * c + m)
                act.activation(qk_full[:], pj_bank[bank][:, :], ACT.Identity, bias=bias,
                               scale=scale).then_inc(full_ready, 1)
                if c > 0:
                    act.wait_ge(stacked[m][(c - 1) % 2], 2 * STACK * b + STACK * ((c - 1) // 2 + 1))
                elif later(b):
                    act.wait_ge(stacked[m][1], 2 * STACK * b)
                act.activation(parts[:, 2 * m, :], pj_bank[bank][:, :], ACT.Identity, bias=bias,
                               scale=scale).then_inc(pj_free[bank], 1)

            def v_high(b, half, t):
                heads = slice(half * HALF, (half + 1) * HALF)
                if half == 0:
                    bank, used = pj_use(("v", t), b)
                    act.wait_ge(pj_free[bank], used + 1)
                if (later(b) or half) and t == 0:
                    if later(b):
                        act.wait_ge(av_full, H * (b - 1) + HALF * (half + 1))
                act.copy(v_parts[:, t, heads, 0, :],
                         v_full[:, t, :].rearrange("p (h d) -> p h d", h=H)[:, heads]).then_inc(vh_ready, 1)

            def exponentials(b, s):
                act.wait_ge(nm_ready, H * b + s + 1)
                if later(b) or s >= 4:
                    act.wait_ge(av_read, H * b + s - 3)
                for i in range(QT):
                    tile = probs[:, s % 2, OFF[i]:OFF[i] + (i + 1) * P]
                    e = act.activation(tile, tile, ACT.Exp, bias=neg_max[:, s % 2, i:i + 1],
                                       scale=slope(s), accum_out=row_sum[:, s % 4, i:i + 1])
                e.then_inc(p_ready, 1)

            def take_turned(b, s, i):
                n = 2 * (i + 1) * P
                act.wait_ge(pt_full, 4 * (H * b + s) + i + 1)
                if i == 2 and (later(b) or s >= 2):
                    act.wait_ge(av_full, H * b + s - 1)
                act.copy(probs_t[:, s % 2, 2 * OFF[i]:2 * OFF[i] + n],
                         pt_bank[i % 2][:, 0:n]).then_inc(pt_free[i % 2], 1)

            def ctx_high(b, c):
                bank, _ = pj_use(("c", c), b)
                act.wait_ge(pj_full, pj_total(("c", c), b))
                if not later(b) and c == 0:
                    act.wait_ge(coef_st, 16 * 2 * ROLES * MATS)
                act.copy(ctx_t[:, 0, c, :], pj_bank[bank][:, :]).then_inc(ch_ready, 1)

            def step(b, s, carry):
                turned = back(b, s, 2)
                if s < H:
                    exponentials(b, s)
                if not later(b) and s == 2:
                    act.wait_ge(pl_ready, 1)
                if turned:
                    take_turned(*turned, 2)
                    take_turned(*turned, 3)
                for key in active(UNITS, s, carry):
                    if key[0] in "qk":
                        qk_high(b + place(key, s), *key)
                for key in active(TURNS, s, carry):
                    (x_high if key[0] == "x" else ctx_high)(b + place(key, s), key[1])
                for half, t in SPLITS.get((s + 1) % H, []) if s < H else []:
                    if s >= HALF - 1 and carry and half == 0:
                        v_high(b + 1, half, t)
                    elif s < HALF - 1:
                        v_high(b, half, t)

            def w_high(n):
                act.wait_ge(w_ld[n % 3], 16 * (n // 3 + 1))
                act.copy(w_piece(w_hi, n), w_raw[:, n % 3]).then_inc(wh_ready, 1)

            act.dma_start(ident[:], c_ident).then_inc(ident_ld, 16)
            w_high(0)
            x_high(0, 0)
            x_high(0, 1)
            w_high(1)
            x_high(0, 2)
            x_high(0, 3)
            for n in range(2, 6):
                w_high(n)
            act.wait_ge(const_ld, 16 * 5)
            act.copy(basis[:], basis_raw)
            act.wait_ge(small_set, 3)
            qk_high(0, "q", 0)
            w_high(6)
            qk_high(0, "k", 0)
            w_high(7)
            act.wait_ge(poly_step, 11)
            act.copy(poly_hi.rearrange("p d e m n -> p (d e m n)"),
                     poly.rearrange("p d e n -> p (d e n)")).then_inc(ph_ready, 1)
            for t in range(2):
                v_high(0, 0, t)
            for s in range(HALF):
                step(0, s, False)
            with act.Fori(1, B) as b:
                for s in range(HALF, H):
                    step(b - 1, s, True)
                for s in range(HALF):
                    step(b, s, True)
            for s in range(HALF, H + 3):
                step(B - 1, s, False)
            ctx_high(B - 1, KC - 1)
            act.activation(warm[:], basis[0:1, 0:1].bitcast(F32), ACT.Silu)

        @block.gpsimd
        def _(pool):
            def inverse_std(b, n):
                two = slice(2 * n, 2 * n + 2)
                pool.wait_ge(ln_var, 2 * b + n + 1)
                pool.tensor_tensor(rstd[:, two], varp[:, two], minus_half[:, two], ALU.pow
                                   ).then_inc(rstd_ready, 1)

            def qk_low(b, name, c):
                m = "qk".index(name)
                bank, used = pj_use((name, c), b)
                pool.wait_ge(pj_free[bank], used + 1)
                pool.tensor_tensor(parts[:, 2 * m + 1, :], qk_full[:], parts[:, 2 * m, :].bitcast(F32),
                                   ALU.subtract).then_inc(ql_ready, 1)

            def probs_low(b, s):
                pool.wait_ge(hi_ready, H * b + s + 1)
                pool.tensor_tensor(probs16[:, s % 2, 1, :], probs[:, s % 2, :], probs16[:, s % 2, 0, :],
                                   ALU.subtract).then_inc(lo_ready, 1)

            def step(b, s, carry, carried):
                halved = back(b, s, 1)
                if carry and s in (9, 10):
                    inverse_std(b + 1, s - 9)
                if halved:
                    probs_low(*halved)
                if s < H and (s or later(b)):
                    for key in active(UNITS, (s - 1) % H, carried):
                        if key[0] in "qk":
                            qk_low(b + place(key, s - 1), *key)

            pool.wait_ge(small_set, 1)
            inverse_std(0, 0)
            inverse_std(0, 1)
            for n in range(4, 6):
                pool.wait_ge(wh_ready, n + 1)
                pool.tensor_tensor(w_piece(w_lo, n), w_raw[:, n % 3], w_piece(w_hi, n).bitcast(F32),
                                   ALU.subtract).then_inc(wl_pool, 1)
            qk_low(0, "k", 0)
            for n in range(6, W_PIECES):
                pool.wait_ge(wh_ready, n + 1)
                pool.tensor_tensor(w_piece(w_lo, n), w_raw[:, n % 3], w_piece(w_hi, n).bitcast(F32),
                                   ALU.subtract).then_inc(wl_pool, 1)
            pool.wait_ge(ph_ready, 1)
            pool.tensor_tensor(poly_lo.rearrange("p d e m n -> p (d e m n)"),
                               poly.rearrange("p d e n -> p (d e n)"),
                               poly_hi.rearrange("p d e m n -> p (d e m n)").bitcast(F32),
                               ALU.subtract).then_inc(pl_ready, 1)
            for s in range(HALF):
                step(0, s, False, False)
            with pool.Fori(1, B) as b:
                for s in range(HALF, H):
                    step(b - 1, s, True, s > HALF)
                for s in range(HALF):
                    step(b, s, True, True)
            for s in range(HALF, H + 1):
                step(B - 1, s, False, False)

        @block.sync
        def _(sp):
            def load_x(b, t):
                sp.dma_start(x_in[:, t, :], rows_of(x_t, QT * b + t)).then_inc(x_ld[t], 16)

            def store_xt(b):
                bank, used = pj_use(("x", QT - 1), b)
                sp.wait_ge(pj_free[bank], used + 1)
                sp.nop(nofuse=True)
                for e, part in enumerate((xt_hi, xt_lo)):
                    sp.dma_start(rows_of(xt_d, 2 * b + e), part[:].rearrange("p c n -> p (c n)").bitcast(F32)
                                 ).then_inc(xt_st, 16)

            def stack(b, c):
                if later(b) or c >= 2:
                    sp.wait_ge(s_full, 64 * b + 16 * (c - 1))
                    sp.nop(nofuse=True)
                for m, stacks in ((0, q_stack), (1, k_stack)):
                    sp.wait_ge(ql_ready, 8 * b + 2 * c + m + 1)
                    sp.nop(nofuse=True)
                    for role, low in enumerate(((0, 1, 0), (0, 0, 1))[m]):
                        sp.dma_start(
                            stacks[role * HD:(role + 1) * HD, c % 2].rearrange("d h n -> d (h n)").bitcast(F32),
                            parts[:, 2 * m + low, :].bitcast(F32)).then_inc(stacked[m][c % 2], 16)

            def load_residual(b, q):
                sp.dma_start(x_in[:, q, :], rows_of(x_t, QT * b + q)).then_inc(res_ld[q], 16)

            def store_sum(b, q):
                bank, used = pj_use(("o", q), b)
                sp.wait_ge(pj_free[bank], used + 1)
                sp.nop(nofuse=True)
                sp.dma_start(rows_of(mid_d, QT * b + q), x_in[:, q, :]).then_inc(res_st[q], 16)

            def load_piece(n):
                m, half = divmod(n, 2)
                if n >= 7:
                    sp.wait_ge(wl_pool, n - 6)
                elif n >= 3:
                    sp.wait_ge(wl_ready, n - 2)
                src = weights[m].rearrange("(c p) n -> p c n", p=P)
                sp.dma_start(w_raw[:, n % 3], src[:, 2 * half:2 * half + 2, :]).then_inc(w_ld[n % 3], 16)

            for t in range(QT):
                load_x(0, t)
            for n in range(2):
                load_piece(n)
            for room, values in ((b_qk[:, 0, :], bq), (b_qk[:, 1, :], bk), (q_scale[:], c_scale),
                                 (basis_raw, c_basis), (bv_all[:], bv.partition_broadcast(P))):
                sp.dma_start(room, values).then_inc(const_ld, 16)
            load_piece(2)
            sp.dma_start(points, win).then_inc(points_ld, 16)
            sp.dma_start(phase, c_phase).then_inc(points_ld, 16)
            sp.dma_start(dist[:], c_dist).then_inc(points_ld, 16)
            for n in range(3, W_PIECES):
                load_piece(n)
            stack(0, 0)
            store_xt(0)
            sp.wait_ge(pl_ready, 1)
            for e in range(2):
                for role, part in enumerate((poly_hi, poly_hi, poly_lo)):
                    for m in range(MATS):
                        sp.dma_start(
                            coef_d[e, 4 * role:4 * role + 4, m, :].rearrange("d (p n) -> p d n", p=P),
                            part[:, :, e, m, :].bitcast(F32)).then_inc(coef_st, 16)
            stack(0, 1)
            sp.wait_ge(coef_st, 16 * 2 * ROLES * MATS)
            stack(0, 2)
            with sp.Fori(1, B) as b:
                for t in range(QT):
                    load_x(b, t)
                stack(b - 1, 3)
                for q in range(QT):
                    sp.wait_ge(pj_full, pj_total(("x", q), b))
                    sp.nop(nofuse=True)
                    load_residual(b - 1, q)
                store_xt(b)
                stack(b, 0)
                stack(b, 1)
                store_sum(b - 1, 0)
                store_sum(b - 1, 1)
                stack(b, 2)
                store_sum(b - 1, 2)
                store_sum(b - 1, 3)
                for q in range(QT):
                    sp.wait_ge(res_st[q], 16 * b)
                sp.nop(nofuse=True)
            for q in range(QT):
                load_residual(B - 1, q)
            stack(B - 1, 3)
            sp.wait_ge(pj_full, pj_total(("k", KC - 1), B - 1))
            sp.wait_ge(v_done, 2 * QT * B)
            for pair in range(2):
                for m in range(MATS):
                    load_coef(sp, pair, pair, m)
                load_mask(sp, pair, pair)
            for q in range(QT):
                store_sum(B - 1, q)



def ffn(nc, sems, psum, basis, w_room, v_room, xt_room, stored, coef, mask, coef_ld, mask_ld, load_coef, load_mask,
        xt_d, mid_d, bo, out_t):
    NT = B * QT
    with ExitStack() as ctx:
        sb = lambda n, s, dt: ctx.enter_context(nc.sbuf_tensor(n, s, dt))
        BATCHES = [B - 1, *range(B - 1)]
        xt_later = sb("xt", [P, B - 1, 2, KC, S], F32R)
        xt = [xt_room, *[xt_later[:, t] for t in range(B - 1)]]
        acc = sb("acc", [P, NT, D], F32)
        w_hi = sb("fw_hi", [P, 2, MATS, PW], F32R)
        w_lo = w_room[:, 1, 1:4].rearrange("p a c n -> p (a c n)").rearrange("p (s m n) -> p s m n", s=2, m=MATS)
        in_hi = w_room[:, 0, 3].rearrange("p (a b) n -> p a b n", a=2)
        in_lo = w_room[:, 1, 0].rearrange("p (a b) n -> p a b n", a=2)
        silu = v_room[:, 2:4]
        inner = sb("inner", [P, 2, S], F32)
        w_new = sb("w_new", [P, 2, 512], F32)
        bo_all = sb("bo_all", [P, D], F32)

        gate_bank, up_bank, down_bank = psum[0:2], psum[2:4], psum[4:6]
        def poly_banks(pair, g):
            return psum[6 - 2 * g:8 - 2 * g] if not later(pair) and g < 3 else psum[6:8]

        def last(pair):
            return isinstance(pair, int) and pair == PAIRS - 1

        GROUPS = MATS * 2

        res_st, xt_st = stored
        xt_ld = sems(ctx, *[f"xt_ld{b}" for b in range(B)])
        acc_ld = sems(ctx, *[f"acc_ld{b}" for b in range(B)])
        (bo_ld, bo_added, ends_full, start_read, w_merged, wh_ready, wl_ready, gate_full, up_full, silu_ready,
         inner_ready, ih_ready, il_ready, down_full, down_added, out_st) = sems(
            ctx, "bo_ld", "bo_added", "ends_full", "start_read", "w_merged", "wh_ready", "wl_ready", "gate_full",
            "up_full", "silu_ready", "inner_ready", "ih_ready", "il_ready", "down_full", "down_added", "out_st")

        block = ctx.enter_context(nc.Block())

        WGEN = {0: (0,), 1: (1, 2), 2: (3, 4), 3: (5,)}

        @block.tensor
        def _(pe):
            def make(pair, g, sl):
                m, half = divmod(g, 2)
                cols = slice(half * 512, (half + 1) * 512)
                if half == 0:
                    pe.wait_ge(coef_ld[sl][m], 16 * pair + 32 - 16 * sl)
                start_bank, end_bank = poly_banks(pair, g)
                if later(pair) or g >= 3:
                    pe.wait_ge(w_merged, GROUPS * pair + g)
                pe.matmul(start_bank[:, :], basis[0:KPOLY, :], coef[0:KPOLY, sl, m, cols], start=True, stop=True)
                pe.matmul(end_bank[:, :], basis[END_ROW:END_ROW + KPOLY, :],
                          coef[END_ROW:END_ROW + KPOLY, sl, m, cols], start=True, stop=True).then_inc(ends_full, 1)

            def gate_or_up(m, pair, sl, t, j):
                k = 4 * pair + t
                if j == 0 and m == 0 and not later(pair) and t:
                    pe.wait_ge(xt_ld[t], 16)
                if t == 0 and j == 0:
                    pe.wait_ge(wl_ready, GROUPS * pair + 2 * (m + 1))
                bank, full = ((gate_bank, gate_full), (up_bank, up_full))[m]
                if later(k):
                    pe.wait_ge((silu_ready, inner_ready)[m], 2 * k + j - 1)
                for q in range(KC):
                    cols = slice(q * 2 * P + j * P, q * 2 * P + (j + 1) * P)
                    hi, lo = w_hi[:, sl, m, cols], w_lo[:, sl, m, cols]
                    pe.matmul(bank[j][:, :], hi, xt[t][:, 0, q, :], start=(q == 0), stop=False)
                    pe.matmul(bank[j][:, :], hi, xt[t][:, 1, q, :], start=False, stop=False)
                    mm = pe.matmul(bank[j][:, :], lo, xt[t][:, 0, q, :], start=False, stop=(q == KC - 1))
                mm.then_inc(full, 1)

            def down(pair, sl, t):
                k = 4 * pair + t
                pe.wait_ge(il_ready, 2 * k + 2)
                if t == 0:
                    pe.wait_ge(wl_ready, GROUPS * pair + GROUPS)
                for i in range(QT):
                    bank = down_bank[i % 2]
                    if later(k) or i >= 2:
                        pe.wait_ge(down_added, QT * k + i - 1)
                    for j in range(2):
                        hi, lo = in_hi[:, t % 2, j, i * P:(i + 1) * P], in_lo[:, t % 2, j, i * P:(i + 1) * P]
                        r_hi, r_lo = [w[:, sl, 2, j * 512:(j + 1) * 512] for w in (w_hi, w_lo)]
                        pe.matmul(bank[:, :], hi, r_hi, start=(j == 0), stop=False)
                        pe.matmul(bank[:, :], hi, r_lo, start=False, stop=False)
                        mm = pe.matmul(bank[:, :], lo, r_hi, start=False, stop=(j == 1))
                    mm.then_inc(down_full, 1)

            def body(it):
                for sl in range(2):
                    pair = 2 * it + sl
                    for t in range(B):
                        k = 4 * pair + t
                        made = WGEN[t] if not last(pair) else ()
                        for m in range(2):
                            for j in range(2):
                                gate_or_up(m, pair, sl, t, j)
                                if not later(k) and 2 * m + j < 3:
                                    make(0, 3 + 2 * m + j, 0)
                        for g in made[:1]:
                            make(pair + 1, g, 1 - sl)
                        if t:
                            down(pair, sl, t - 1)
                        elif later(k):
                            down(pair - 1, 1 - sl, B - 1)
                        for g in made[1:]:
                            make(pair + 1, g, 1 - sl)

            for g in range(3):
                make(0, g, 0)
            body(0)
            with pe.Fori(1, PAIRS // 2 - 1) as it:
                body(it)
            body(PAIRS // 2 - 1)
            down(PAIRS - 1, 1, B - 1)

        @block.scalar
        def _(act):
            def start_part(pair, g):
                act.wait_ge(ends_full, GROUPS * pair + g + 1)
                start_bank, _ = poly_banks(pair, g)
                if later(pair) or g >= 2:
                    act.wait_ge(wl_ready, GROUPS * pair + g - 1)
                act.copy(w_new[:, g % 2, :], start_bank[:, :]).then_inc(start_read, 1)

            def high(pair, g, sl):
                m, half = divmod(g, 2)
                act.wait_ge(w_merged, GROUPS * pair + g + 1)
                act.copy(w_hi[:, sl, m, half * 512:(half + 1) * 512], w_new[:, g % 2, :]).then_inc(wh_ready, 1)

            def gated(k, t, j):
                act.wait_ge(gate_full, 2 * k + j + 1)
                if later(k):
                    act.wait_ge(inner_ready, 2 * k + j - 1)
                act.activation(silu[:, j, :], gate_bank[j][:, :], ACT.Silu).then_inc(silu_ready, 1)

            def inner_high(k, t, j):
                act.wait_ge(inner_ready, 2 * k + j + 1)
                if not isinstance(k, int) or k >= 2:
                    act.wait_ge(down_full, QT * (k - 1))
                act.copy(in_hi[:, t % 2, j, :], inner[:, j, :]).then_inc(ih_ready, 1)

            def body(it):
                for sl in range(2):
                    pair = 2 * it + sl
                    for t in range(B):
                        k = 4 * pair + t
                        made = WGEN[t] if not last(pair) else ()
                        for j in range(2):
                            gated(k, t, j)
                            if not later(k):
                                start_part(0, 3 + j)
                                high(0, 3 + j, 0)
                        if not later(k):
                            start_part(0, 5)
                            high(0, 5, 0)
                        for j in range(2):
                            inner_high(k, t, j)
                        for g in made:
                            start_part(pair + 1, g)
                            high(pair + 1, g, 1 - sl)

            start_part(0, 0)
            start_part(0, 1)
            high(0, 0, 0)
            high(0, 1, 0)
            start_part(0, 2)
            high(0, 2, 0)
            body(0)
            with act.Fori(1, PAIRS // 2 - 1) as it:
                body(it)
            body(PAIRS // 2 - 1)

        @block.vector
        def _(dve):
            def merge(pair, g, sl):
                m, half = divmod(g, 2)
                if g == 0:
                    dve.wait_ge(mask_ld[sl], 8 * pair + 16 - 8 * sl)
                    dve.nop(nofuse=True)
                dve.wait_ge(start_read, GROUPS * pair + g + 1)
                dve.nop(nofuse=True)
                _, end_bank = poly_banks(pair, g)
                dve.copy_predicated(w_new[:, g % 2, :], mask[:, sl, m // 2, half * 512:(half + 1) * 512],
                                    end_bank[:, :]).then_inc(w_merged, 1)

            def low(pair, g, sl):
                m, half = divmod(g, 2)
                cols = slice(half * 512, (half + 1) * 512)
                dve.wait_ge(wh_ready, GROUPS * pair + g + 1)
                dve.tensor_tensor(w_lo[:, sl, m, cols], w_new[:, g % 2, :], w_hi[:, sl, m, cols].bitcast(F32),
                                  ALU.subtract).then_inc(wl_ready, 1)

            def multiply(k, t, j):
                dve.wait_ge(silu_ready, 2 * k + j + 1)
                dve.wait_ge(up_full, 2 * k + j + 1)
                if later(k):
                    dve.wait_ge(il_ready, 2 * k + j - 1)
                dve.tensor_tensor(inner[:, j, :], up_bank[j][:, :], silu[:, j, :], ALU.mult
                                  ).then_inc(inner_ready, 1)

            def add_down(pair, t, tiles):
                k = 4 * pair + t
                if not later(pair) and tiles[0] == 0:
                    dve.wait_ge(acc_ld[t], 16 * QT)
                    dve.wait_ge(bo_added, QT * (t + 1))
                for i in tiles:
                    at = acc[:, QT * t + i, :]
                    dve.wait_ge(down_full, QT * k + i + 1)
                    dve.tensor_tensor(at, down_bank[i % 2][:, :], at, ALU.add).then_inc(down_added, 1)

            def body(it):
                for sl in range(2):
                    pair = 2 * it + sl
                    for t in range(B):
                        k = 4 * pair + t
                        made = WGEN[t] if not last(pair) else ()
                        if not later(k):
                            for g in range(3, GROUPS):
                                merge(0, g, 0)
                                low(0, g, 0)
                        for j in range(2):
                            multiply(k, t, j)
                        done = (pair, t - 1) if t else (pair - 1, B - 1)
                        if later(k):
                            add_down(*done, (0,))
                        for g in made[:1]:
                            merge(pair + 1, g, 1 - sl)
                        if later(k):
                            add_down(*done, (1,))
                        for g in made[:1]:
                            low(pair + 1, g, 1 - sl)
                        if later(k):
                            add_down(*done, (2, 3))
                        for g in made[1:]:
                            merge(pair + 1, g, 1 - sl)
                            low(pair + 1, g, 1 - sl)

            merge(0, 0, 0)
            merge(0, 1, 0)
            low(0, 0, 0)
            low(0, 1, 0)
            merge(0, 2, 0)
            low(0, 2, 0)
            body(0)
            with dve.Fori(1, PAIRS // 2 - 1) as it:
                body(it)
            body(PAIRS // 2 - 1)
            add_down(PAIRS - 1, B - 1, range(QT))

        @block.gpsimd
        def _(pool):
            def inner_low(k, t, j):
                pool.wait_ge(ih_ready, 2 * k + j + 1)
                if not isinstance(k, int) or k >= 2:
                    pool.wait_ge(down_full, QT * (k - 1))
                pool.tensor_tensor(in_lo[:, t % 2, j, :], inner[:, j, :], in_hi[:, t % 2, j, :].bitcast(F32),
                                   ALU.subtract).then_inc(il_ready, 1)

            def body(it):
                for sl in range(2):
                    pair = 2 * it + sl
                    for t in range(B):
                        for j in range(2):
                            inner_low(4 * pair + t, t, j)
                        if isinstance(pair, int) and pair == 0:
                            pool.wait_ge(bo_ld, 16)
                            pool.wait_ge(acc_ld[t], 16 * QT)
                            for i in range(QT):
                                at = acc[:, QT * t + i, :]
                                pool.tensor_tensor(at, at, bo_all[:], ALU.add).then_inc(bo_added, 1)

            body(0)
            with pool.Fori(1, PAIRS // 2) as it:
                body(it)

        @block.sync
        def _(sp):
            def load_weights(pair, sl):
                for m in range(MATS):
                    sp.wait_ge(ends_full, GROUPS * (pair - 2) + 2 * (m + 1))
                    sp.nop(nofuse=True)
                    load_coef(sp, pair, sl, m)
                sp.wait_ge(w_merged, GROUPS * (pair - 1))
                sp.nop(nofuse=True)
                load_mask(sp, pair, sl)

            def body(it):
                for sl in range(2):
                    load_weights(2 * it + sl + 2, sl)

            sp.wait_ge(xt_st, 32 * B)
            for q in range(QT):
                sp.wait_ge(res_st[q], 16 * B)
            for t in range(1, B):
                b = BATCHES[t]
                sp.dma_start(xt[t].rearrange("p e c n -> p e (c n)").bitcast(F32),
                             xt_d[2 * b:2 * b + 2].rearrange("e p n -> p e n")).then_inc(xt_ld[t], 16)
            sp.dma_start(bo_all[:], bo.partition_broadcast(P)).then_inc(bo_ld, 16)
            for n in range(NT):
                t, q = divmod(n, QT)
                sp.dma_start(acc[:, n, :], mid_d[QT * BATCHES[t] + q]).then_inc(acc_ld[t], 16)
            body(0)
            with sp.Fori(1, PAIRS // 2 - 1) as it:
                body(it)
            for n in range(NT):
                sp.wait_ge(down_added, QT * B * (PAIRS - 1) + n + 1)
                t, q = divmod(n, QT)
                sp.dma_start(out_t[QT * BATCHES[t] + q], acc[:, n, :]).then_inc(out_st, 16)
            sp.wait_ge(out_st, 16 * NT)


_INS = ["x", "Wq", "Wk", "Wv", "Wo", "bq", "bk", "bv", "bo"]


def kernel(**inputs):
    import concourse.bacc as _bacc
    from concourse.bass_utils import run_bass_kernel_spmd as _run

    nc = _bacc.Bacc("TRN2", target_bir_lowering=False, num_devices=1)
    arrays = {n: np.ascontiguousarray(inputs[f"L0_attn_{n}"]) for n in _INS}
    for n in ("Wq", "Wk", "bq", "bk"):
        w = arrays[n]
        arrays[n] = np.ascontiguousarray(w.reshape(-1, KC, HPC, HD).swapaxes(2, 3).reshape(w.shape))
    for n in ("bq", "bk"):
        arrays[n] = np.ascontiguousarray(arrays[n].reshape(KC, P).T)
    arrays["windows"] = control_windows([np.asarray(inputs[f"L0_ffn_{n}_cp"]) for n in ("gate", "up", "down")])
    arrays.update(shape_constants())
    order = [*_INS, "windows", "c_basis", "c_phase", "c_mask", "c_dist", "c_ident", "c_scale"]
    args = [nc.dram_tensor(n, arrays[n].shape, mybir.dt.from_np(arrays[n].dtype), kind="ExternalInput").ap()
            for n in order]
    result = nc.dram_tensor("result", (B, S, D), F32, kind="ExternalOutput").ap()
    build_kernel(nc, *args, result)
    r = _run(nc, [arrays], core_ids=[0])
    return r.results[0]["result"]
```
